# Optimizing a Trainium2 kernel written in Bass

```python
import numpy as np
import jax
import jax.numpy as jnp

def _softmax(x, axis=-1):
    return jax.nn.softmax(x, axis=axis)

def _gelu(x):
    return jax.nn.gelu(x, approximate=True)

def _silu(x):
    return jax.nn.silu(x)

def _sigmoid(x):
    return jax.nn.sigmoid(x)

def _layernorm(x, axis=-1, eps=1e-05):
    m = jnp.mean(x, axis=axis, keepdims=True)
    v = jnp.var(x, axis=axis, keepdims=True)
    return (x - m) / jnp.sqrt(v + eps)

def _scatter_add(tgt, idx, src, axis=0):
    return tgt.at[idx].add(src)

def _segment_sum(src, seg, n):
    return jax.ops.segment_sum(src, seg, n)
kernel_name = 'mk_adj_resnorm_d2_adj_r2_8f942a'

def setup_inputs(seed: int=0):
    np.random.seed(seed)
    _w = jnp.asarray

    def _rec_inputs():
        import jax
        import jax.numpy as jnp
        _gk = jax.random.key(seed)
        x = -0.000929 + 1 * jax.random.normal(jax.random.fold_in(_gk, 1), (8192, 128), jnp.float32)
        _a = jax.random.bernoulli(jax.random.fold_in(_gk, 2), 0.000244141, (8192, 8192))
        _a = jnp.logical_or(_a, jnp.swapaxes(_a, -1, -2))
        _a = jnp.logical_or(_a, jnp.eye(8192, dtype=bool))
        _af = _a.astype(jnp.float32)
        adj = _af
        return (x, adj)
    x, adj = _rec_inputs()

    def _L0_gnn_setup():
        import jax, jax.numpy as jnp
        import numpy as np
        N = 4096
        F_IN = 128
        H = 2
        DH = 64
        NEG = -1000000000.0
        key = jax.random.key(seed)
        k1, k2, k3, k4, k5 = jax.random.split(key, 5)
        node_features = jax.random.normal(k1, (N, F_IN), dtype=jnp.float32)
        adj = (jax.random.uniform(k2, (N, N)) < 32.0 / N).astype(jnp.float32)
        adj = jnp.maximum(adj, jnp.eye(N, dtype=jnp.float32))
        W = jax.random.normal(k3, (H, F_IN, DH), dtype=jnp.float32) * 0.1
        a_self = jax.random.normal(k4, (H, DH), dtype=jnp.float32) * 0.1
        a_neigh = jax.random.normal(k5, (H, DH), dtype=jnp.float32) * 0.1
        bias = jnp.zeros((H * DH,), dtype=jnp.float32)
        return {'node_features': node_features, 'adj_matrix': adj, 'W': W, 'a_self': a_self, 'a_neigh': a_neigh, 'bias': bias}
    _L0_gnn_all = _L0_gnn_setup()
    _L0_gnn_in = {k: v for k, v in _L0_gnn_all.items() if k in ('W', 'a_self', 'a_neigh', 'bias')}
    del _L0_gnn_all

    def _L1_gnn_setup():
        import jax, jax.numpy as jnp
        import numpy as np
        N, D = (4096, 128)
        EDGE_PROB = 0.005
        COS_EPS = 1e-08
        key = jax.random.key(seed)
        kx, ka = jax.random.split(key)
        x = jax.random.normal(kx, (N, D), dtype=jnp.float32)
        adj = (jax.random.uniform(ka, (N, N)) < EDGE_PROB).astype(jnp.float32)
        return {'t': jnp.float32(0.0), 'x': x, 'adj': adj, 'alpha': jnp.float32(0.5), 'beta': jnp.float32(1.0)}
    _L1_gnn_all = _L1_gnn_setup()
    _L1_gnn_in = {k: v for k, v in _L1_gnn_all.items() if k in ('t', 'alpha', 'beta')}
    del _L1_gnn_all
    return {'x': x, 'adj': adj, 'L0_gnn_W': _L0_gnn_in['W'], 'L0_gnn_a_self': _L0_gnn_in['a_self'], 'L0_gnn_a_neigh': _L0_gnn_in['a_neigh'], 'L0_gnn_bias': _L0_gnn_in['bias'], 'L1_gnn_t': _L1_gnn_in['t'], 'L1_gnn_alpha': _L1_gnn_in['alpha'], 'L1_gnn_beta': _L1_gnn_in['beta']}

def reference(x, adj, L0_gnn_W, L0_gnn_a_self, L0_gnn_a_neigh, L0_gnn_bias, L1_gnn_t, L1_gnn_alpha, L1_gnn_beta):
    import jax
    import jax.numpy as jnp

    def _L0_gnn_ref(node_features, adj_matrix, W, a_self, a_neigh, bias):
        import jax, jax.numpy as jnp
        import numpy as np
        N = 4096
        F_IN = 128
        H = 2
        DH = 64
        NEG = -1000000000.0
        h = jnp.einsum('nf,hfd->hnd', node_features, W)
        s_self = jnp.einsum('hnd,hd->hn', h, a_self)
        s_neigh = jnp.einsum('hnd,hd->hn', h, a_neigh)
        scores = s_self[:, :, None] + s_neigh[:, None, :]
        scores = scores + (1.0 - adj_matrix)[None] * NEG
        attn = jax.nn.softmax(scores, axis=-1)
        ctx = jnp.einsum('hij,hjd->hid', attn, h)
        out = jnp.transpose(ctx, (1, 0, 2)).reshape(node_features.shape[0], -1)
        out = out + bias
        return jax.nn.elu(out)

    def _L1_gnn_ref(t, x, adj, alpha, beta):
        import jax, jax.numpy as jnp
        import numpy as np
        N, D = (4096, 128)
        EDGE_PROB = 0.005
        COS_EPS = 1e-08
        deg = jnp.clip(adj.sum(axis=1), 1.0)
        dis = deg ** (-0.5)
        adj_norm = dis[:, None] * adj * dis[None, :]
        diffusion = adj_norm @ x - x
        norms = jnp.maximum(jnp.linalg.norm(x, axis=-1), COS_EPS)
        sim = x @ x.T / (norms[:, None] * norms[None, :])
        attn = jax.nn.softmax(beta * sim * adj, axis=1)
        attn = jax.lax.stop_gradient(attn)
        return diffusion + jax.nn.sigmoid(alpha) * (attn @ x - x)
    x = _layernorm(x + _L0_gnn_ref(x, adj, L0_gnn_W, L0_gnn_a_self, L0_gnn_a_neigh, L0_gnn_bias), axis=-1)
    x = _layernorm(x + _L1_gnn_ref(L1_gnn_t, x, adj, L1_gnn_alpha, L1_gnn_beta), axis=-1)
    return x

_drawn_inputs = setup_inputs


def setup_inputs(seed=0):
    import zlib

    import numpy as np

    out = dict(_drawn_inputs(seed))
    spreads = {'L0_gnn_bias': (0.0, 0.1)}
    factors = {}
    for name, (base, spread) in spreads.items():
        noise = np.random.default_rng([zlib.crc32(name.encode()), seed]).standard_normal(out[name].shape)
        drawn = base * np.exp(spread * noise) if base else spread * noise
        out[name] = jnp.asarray(drawn.astype(out[name].dtype))
    for name, factor in factors.items():
        out[name] = (out[name] * factor).astype(out[name].dtype)
    return out
```

```python
from contextlib import ExitStack

import concourse.bass as bass
from concourse import mybir
from concourse.alu_op_type import AluOpType as ALU

ACT = mybir.ActivationFunctionType
F32 = mybir.dt.float32
F16 = mybir.dt.float16
BF16 = mybir.dt.bfloat16
AX_X = mybir.AxisListType.X
RMAX = bass.bass_isa.ReduceOp.max

P = 128
LN_EPS = 1e-5
NORM_FLOOR = 1e-8

SPLIT = 4096.0


def graph_layers_kernel(nc, x, adj, W, a_self, a_neigh, bias, t_in, alpha, beta, out):
    N, D = x.shape
    H, _, DH = W.shape
    NT = N // P
    GB = 4
    GW = GB * P
    NG = N // GW
    CJ = 4
    RING = 4
    CYC = CJ * RING
    TURNS = NT // CYC
    WC = D + H
    VC = 3 * WC + 1
    XC = 2 * D + 2
    DC = 2 * D
    AC = DC + D + 1
    AHEAD = 3
    SB = 4
    NE = 4
    NH = 4
    QT = 4
    NQ = NT // QT
    assert D == P and H * DH == D and NG * GW == N and TURNS * CYC == NT and NG % 2 == 0

    adj_chunks = adj.rearrange("(c t p) (g w) -> g c p t w", t=CJ, p=P, w=GW)
    x_quarters = x.rearrange("(k t p) f -> k p t f", k=4, p=P)
    out_groups = out.rearrange("(g b p) f -> g p b f", b=GB, p=P)

    with ExitStack() as ctx:
        def sb(name, shape, dt):
            return ctx.enter_context(nc.sbuf_tensor(name, shape, dt))

        def sem(name):
            return ctx.enter_context(nc.semaphore(name))

        psum = ctx.enter_context(nc.psum_tensor("psum", [P, 8, 512], F32))

        ring = sb("ring", [P, RING, CJ, GW], F32)
        ring_bf = ring[:].bitcast(BF16).rearrange("p r t (w e) -> p r t w e", e=2)
        nodes = sb("nodes", [P, NT, D], F32)
        table = sb("table", [P, NT * (VC + 1)], BF16)
        V = table[:].rearrange("p (t c) -> p t c", c=VC + 1)
        dx = table[:, 0:NT * DC].bitcast(F16).rearrange("p (t c) -> p t c", c=DC)
        wide = sb("wide", [P, NT * WC], F32)
        G = wide[:].rearrange("p (t c) -> p t c", c=WC)
        xsplit = wide[:].bitcast(F16)[:, 0:NT * XC].rearrange("p (t c) -> p t c", c=XC)
        unit_hi = sb("unit_hi", [P, N], F16)
        unit_lo = sb("unit_lo", [P, N], F16)
        edge = sb("edge", [P, NE, GW], F32)
        edge_hi = sb("edge_hi", [P, NH, GW], F16)
        edge_lo = sb("edge_lo", [P, NH, GW], F16)
        xT = edge
        ta = sb("ta", [P, GB, D], F32)
        tb = sb("tb", [P, GB, D], F32)
        tc = sb("tc", [P, GB, D], F32)
        u = sb("u", [P, GB, WC], F32)
        ident = sb("ident", [P, P], F32)
        Wx = sb("Wx", [P, WC], F32)
        zeros = sb("zeros", [P, 512], BF16)
        ones16 = sb("ones16", [P, P], F16)
        bias_bc = sb("bias_bc", [P, D], F32)
        total_bc = sb("total_bc", [P, D], F32)
        a_bc = bias_bc
        deg = sb("deg", [P, NT], F32)
        dis = sb("dis", [P, NT], F32)
        rnorm = sb("rnorm", [P, NT], F32)
        sm = sb("sm", [P, 40], F32)
        smax, negmax = sm[:, 0:H], sm[:, 2:2 + H]
        alpha_t, beta_t = sm[:, 4:5], sm[:, 5:6]
        neg_beta, neg_abs, c0 = sm[:, 6:7], sm[:, 7:8], sm[:, 8:9]
        beta_scale, sig, neg_sig, n_c0, sig_s = sm[:, 9:10], sm[:, 10:11], sm[:, 11:12], sm[:, 12:13], sm[:, 13:14]
        mean, ss, var, rstd, nn = (sm[:, 16 + 4 * i:20 + 4 * i] for i in range(5))
        gmax = sm[:, 36:36 + H]
        dx_f = (ta, tb)
        unit_f = (tc[:], u[:, :, 0:D])
        rden = sb("rden", [P, GB, H], F32)
        mhalf = sb("mhalf", [P, NT], F32)

        x_in = [sem(f"x_in{k}") for k in range(4)]
        w_in = sem("w_in")
        a_in = sem("a_in")
        bias_in = sem("bias_in")
        ab_in = sem("ab_in")
        chunk_in = [sem(f"chunk_in{s}") for s in range(RING)]
        chunk_free = sem("chunk_free")
        consts = sem("consts")
        wx_ready = sem("wx_ready")
        xT_ps = sem("xT_ps")
        xT_sb = sem("xT_sb")
        h_ps = sem("h_ps")
        h_sb = sem("h_sb")
        smax_ready = sem("smax_ready")
        gmax_ready = sem("gmax_ready")
        negmax_ready = sem("negmax_ready")
        e_ready = sem("e_ready")
        eh_ready = sem("eh_ready")
        part_hi = sem("part_hi")
        rest1 = sem("rest1")
        part_mid = sem("part_mid")
        table_ready = sem("table_ready")
        scal_ready = sem("scal_ready")
        scal_exp = sem("scal_exp")
        sums_ready = sem("sums_ready")
        sums_free = sem("sums_free")
        elu_in = sem("elu_in")
        elu_exp = sem("elu_exp")
        var_ready = sem("var_ready")
        rstd_ready = sem("rstd_ready")
        norm_in = sem("norm_in")
        norm_pow = sem("norm_pow")
        x1_ready = sem("x1_ready")
        x1_hi = sem("x1_hi")
        x1_lo = sem("x1_lo")
        all_norms = sem("all_norms")
        unit_f32 = sem("unit_f32")
        unit_ps = sem("unit_ps")
        unit_hi_ready = sem("unit_hi_ready")
        unit_ready = sem("unit_ready")
        dx_f32 = sem("dx_f32")
        dx_hi_ready = sem("dx_hi_ready")
        dx_ready = sem("dx_ready")
        total_ps = sem("total_ps")
        total_read = sem("total_read")
        score_ps = sem("score_ps")
        score_exp = sem("score_exp")
        edge_ready = sem("edge_ready")
        hi_ready = sem("hi_ready")
        lo_ready = sem("lo_ready")
        split_free = sem("split_free")
        acc_ready = sem("acc_ready")
        diff_summed = sem("diff_summed")
        u_free = sem("u_free")
        att_copied = sem("att_copied")
        out_ready = sem("out_ready")
        stored = sem("stored")
        row_free = sem("row_free")
        dis_ready = sem("dis_ready")
        dve_chain = sem("dve_chain")

        acc = psum[:, 0:GB, :]

        block = ctx.enter_context(nc.Block())

        @block.sync
        def _(sp):
            sp.dma_start(Wx[:, 0:D].rearrange("p (h d) -> p h d", h=H),
                         W.rearrange("h f d -> f h d")).then_inc(w_in, 16)
            sp.dma_start(a_bc[:], a_neigh.rearrange("h d -> (h d)").partition_broadcast(P)).then_inc(a_in, 16)
            sp.dma_start(alpha_t, alpha.rearrange("a b -> (a b)").partition_broadcast(P)).then_inc(ab_in, 16)
            sp.dma_start(beta_t, beta.rearrange("a b -> (a b)").partition_broadcast(P)).then_inc(ab_in, 16)
            for k in range(4):
                sp.dma_start(nodes[:, k * (NT // 4):(k + 1) * (NT // 4), :], x_quarters[k]).then_inc(x_in[k], 16)
            sp.wait_ge(wx_ready, 1)
            sp.dma_start(bias_bc[:], bias.partition_broadcast(P)).then_inc(bias_in, 16)
            for layer in range(2):
                with sp.Fori(0, NG) as g:
                    with sp.Fori(0, TURNS) as turn:
                        for s in range(RING):
                            sp.wait_ge(chunk_free, layer * NG * TURNS * RING + (g * TURNS + turn) * RING + s + 1)
                            sp.dma_start(ring[:, s], adj_chunks[g, turn * RING + s]).then_inc(chunk_in[s], 16)

        @block.gpsimd
        def _(pool):
            pool.memset(mhalf[:], -0.5).then_inc(consts, 1)
            pool.memset(ones16[:], 1.0).then_inc(consts, 1)
            pool.memset(zeros[:], 0.0).then_inc(consts, 1)
            pool.memset(ident[:], 0.0).then_inc(consts, 1)
            pool.wait_ge(consts, 4)
            pool.affine_select(out=ident[:], in_=ident[:], compare_op=ALU.not_equal, fill=1.0, base=0,
                               pattern=[[-1, P]], channel_multiplier=1).then_inc(consts, 1)
            pool.wait_ge(smax_ready, 1)
            pool.partition_all_reduce(gmax, smax, P, RMAX).then_inc(gmax_ready, 1)
            with pool.Fori(0, NG) as g:
                tiles = bass.ds(g * GB, GB)
                pool.wait_ge(var_ready, g + 1)
                pool.tensor_tensor(rstd, var, mhalf[:, 0:GB], ALU.pow).then_inc(rstd_ready, 1)
                pool.tensor_tensor(dis[:, tiles], deg[:, tiles], mhalf[:, 0:GB], ALU.pow).then_inc(dis_ready, 1)
                pool.wait_ge(norm_in, g + 1)
                pool.tensor_tensor(rnorm[:, tiles], nn, mhalf[:, 0:GB], ALU.pow).then_inc(norm_pow, 1)
            pool.wait_ge(all_norms, 1)
            with pool.Fori(0, NQ // 2) as q2:
                for b in range(2):
                    tiles = bass.ds((q2 * 2 + b) * QT, QT)
                    pool.wait_ge(unit_ps, q2 * 2 + 1)
                    pool.tensor_tensor(unit_f[b], nodes[:, tiles, :],
                                       rnorm[:, tiles].unsqueeze(2).broadcast_to([P, QT, D]),
                                       ALU.mult).then_inc(unit_f32, 1)
            with pool.Fori(0, NG) as g:
                pool.wait_ge(var_ready, g + NG + 1)
                pool.tensor_tensor(rstd, var, mhalf[:, 0:GB], ALU.pow).then_inc(rstd_ready, 1)
                pool.wait_ge(out_ready, g + 1)
                pool.dma_start(out_groups[g], tb[:]).then_inc(stored, 16)
                pool.wait_ge(stored, g * 16 + 16)
                pool.sem_inc(row_free, 1)
            pool.wait_ge(stored, 16 * NG)

        @block.scalar
        def _(act):
            with act.Fori(0, NQ // 2) as q2:
                act.wait_ge(h_ps, q2 * 2 + 1)
                for b in range(2):
                    act.wait_ge(xT_ps, q2 * 2 + b + 1)
                    act.activation(xT[:, b, :], psum[:, b, :], ACT.Copy).then_inc(xT_sb, 1)
            act.wait_ge(scal_ready, 1)
            act.activation(c0, neg_abs, ACT.Exp).then_inc(scal_exp, 1)
            act.activation(sig, alpha_t, ACT.Exp, scale=-1.0).then_inc(scal_exp, 1)
            act.wait_ge(negmax_ready, 1)
            for h in range(H):
                act.activation(G[:, :, D + h], G[:, :, D + h], ACT.Exp, bias=negmax[:, h:h + 1]).then_inc(e_ready, 1)
            for k in range(TURNS):
                tiles = slice(k * CYC, (k + 1) * CYC)
                act.wait_ge(eh_ready, k + 1)
                act.activation(V[:, tiles, 0:WC], G[:, tiles, :], ACT.Copy).then_inc(part_hi, 1)
                act.wait_ge(rest1, k + 1)
                act.activation(V[:, tiles, WC:2 * WC], G[:, tiles, :], ACT.Copy).then_inc(part_mid, 1)
            with act.Fori(0, NG) as g:
                tiles = bass.ds(g * GB, GB)
                act.wait_ge(elu_in, g + 1)
                act.activation(tb[:], tb[:], ACT.Exp).then_inc(elu_exp, 1)
                act.wait_ge(x1_ready, g + 1)
                act.activation(xsplit[:, tiles, 0:D], nodes[:, tiles, :], ACT.Copy,
                               scale=SPLIT).then_inc(x1_hi, 1)
            with act.Fori(0, NQ // 2) as q2:
                for b in range(2):
                    q = q2 * 2 + b
                    act.wait_ge(dx_f32, q + 1)
                    act.activation(dx[:, bass.ds(q * QT, QT), 0:D], dx_f[b][:], ACT.Copy,
                                   scale=SPLIT).then_inc(dx_hi_ready, 1)
                    act.wait_ge(unit_ps, q + 2)
                    act.activation(unit_hi[:, bass.ds(q * QT * P, QT * P)], psum[:, GB + b, :], ACT.Copy,
                                   scale=SPLIT).then_inc(unit_hi_ready, 1)

            def exp_scores(bank, n):
                act.wait_ge(score_ps, n + 1)
                act.activation(psum[:, GB + bank, :], psum[:, GB + bank, :], ACT.Exp, bias=neg_abs,
                               scale=beta_scale).then_inc(score_exp, 1)

            exp_scores(0, 0)
            with act.Fori(0, NG) as g:
                with act.Fori(0, TURNS) as turn:
                    base = act.snap((g * TURNS + turn) * CYC)
                    for k in range(CYC):
                        exp_scores((k + 1) % SB, base + k + 1)
                        act.wait_ge(edge_ready, base + k + 2)
                        act.wait_ge(split_free, base + k + 1)
                        act.activation(edge_hi[:, k % NH, :], edge[:, k % NE, :], ACT.Copy).then_inc(hi_ready, 1)
                act.wait_ge(diff_summed, g + 2)
                act.wait_ge(u_free, g + 1)
                act.activation(u[:, :, 0:D + 1], acc[:, :, DC:AC], ACT.Copy).then_inc(att_copied, 1)

        @block.tensor
        def _(pe):
            pe.sem_inc(chunk_free, RING)
            pe.sem_inc(sums_free, 2)
            pe.sem_inc(split_free, NH)
            for start in (h_ps, unit_ps, unit_ready, dx_ready, diff_summed, att_copied, edge_ready, lo_ready, row_free):
                pe.sem_inc(start, 1)
            pe.wait_ge(consts, 5)
            pe.wait_ge(wx_ready, 1)
            for q2 in range(NQ // 2):
                pe.wait_ge(x_in[q2 // 2], 16)
                for b in range(2):
                    for t in range(QT):
                        last = nc.tensor.transpose(psum[:, b, t * P:(t + 1) * P], nodes[:, (q2 * 2 + b) * QT + t, :],
                                                   ident[:])
                    last.then_inc(xT_ps, 1)
                if q2:
                    pe.wait_ge(h_sb, q2 * 2)
                for b in range(2):
                    pe.wait_ge(xT_sb, q2 * 2 + b + 1)
                    for t in range(QT):
                        c = (t % 2) * 256
                        last = nc.tensor.matmul(psum[:, 2 + 2 * b + t // 2, c:c + WC],
                                                xT[:, b, t * P:(t + 1) * P], Wx[:], start=True, stop=True)
                    last.then_inc(h_ps, 1)
            pe.wait_ge(h_sb, NQ)

            def sweep(bank, cols, first):
                return nc.tensor.matmul(psum[:, bank, 0:cols], zeros[:, 0:P], zeros[:, 0:cols],
                                        start=first, stop=not first, skip_group_check=True)

            with pe.Fori(0, NG // 2) as g2:
                for half in range(2):
                    g = g2 * 2 + half
                    pe.wait_ge(sums_free, g + 1)
                    for b in range(GB):
                        sweep(half * GB + b, VC, True)
                    with pe.Fori(0, TURNS) as turn:
                        pe.wait_ge(table_ready, turn + 1)
                        for s in range(RING):
                            pe.wait_ge(chunk_in[s], (g * TURNS + turn + 1) * 16)
                            for t in range(CJ):
                                for b in range(GB):
                                    last = nc.tensor.matmul(psum[:, half * GB + b, 0:VC],
                                                            ring_bf[:, s, t, b * P:(b + 1) * P, 1],
                                                            V[:, turn * CYC + s * CJ + t, 0:VC],
                                                            start=False, stop=False, skip_group_check=True)
                            last.then_inc(chunk_free, 1)
                    for b in range(GB):
                        last = sweep(half * GB + b, VC, False)
                    last.then_inc(sums_ready, 1)
            pe.wait_ge(x1_lo, NG)
            pe.wait_ge(sums_free, NG + 2)
            sweep(0, D, True)
            with pe.Fori(0, NQ) as q:
                for t in range(QT):
                    for part in (0, D + 1):
                        nc.tensor.matmul(psum[:, 0, 0:D], ones16[:], xsplit[:, q * QT + t, part:part + D],
                                         start=False, stop=False, skip_group_check=True)
            sweep(0, D, False).then_inc(total_ps, 1)
            with pe.Fori(0, NQ // 2) as q2:
                pe.wait_ge(unit_ready, q2 * 2 + 1)
                for b in range(2):
                    pe.wait_ge(unit_f32, q2 * 2 + b + 1)
                    for t in range(QT):
                        last = nc.tensor.transpose(psum[:, GB + b, t * P:(t + 1) * P], unit_f[b][:, t, :], ident[:])
                    last.then_inc(unit_ps, 1)
            pe.wait_ge(unit_ready, NQ + 1)
            pe.wait_ge(dx_ready, NQ + 1)
            pe.wait_ge(total_read, 1)

            def scores(bank, tile, group):
                hi_j, lo_j = (part[:, bass.ds(tile * P, P)] for part in (unit_hi, unit_lo))
                hi_i, lo_i = (part[:, bass.ds(group * GW, GW)] for part in (unit_hi, unit_lo))
                nc.tensor.matmul(psum[:, GB + bank, :], hi_j, hi_i, start=True, stop=False)
                nc.tensor.matmul(psum[:, GB + bank, :], hi_j, lo_i, start=False, stop=False)
                nc.tensor.matmul(psum[:, GB + bank, :], lo_j, hi_i, start=False, stop=True).then_inc(score_ps, 1)

            for n in range(AHEAD):
                scores(n, n, 0)
            with pe.Fori(0, NG) as g:
                pe.wait_ge(diff_summed, g + 1)
                pe.wait_ge(att_copied, g + 1)
                for b in range(GB):
                    sweep(b, AC, True)
                with pe.Fori(0, TURNS) as turn:
                    base = pe.snap((g * TURNS + turn) * CYC)
                    next_turn = pe.snap((turn + 1) % TURNS)
                    next_group = pe.snap((g + (turn + 1) // TURNS) % NG)
                    for s in range(RING):
                        pe.wait_ge(chunk_in[s], (g * TURNS + turn + NG * TURNS + 1) * 16)
                        for t in range(CJ):
                            k = s * CJ + t
                            pe.wait_ge(edge_ready, base + k + 1)
                            if k + AHEAD < CYC:
                                scores((k + AHEAD) % SB, turn * CYC + k + AHEAD, g)
                            else:
                                scores((k + AHEAD) % SB, next_turn * CYC + k + AHEAD - CYC, next_group)
                            j = turn * CYC + k
                            for b in range(GB):
                                nc.tensor.matmul(psum[:, b, 0:DC], ring_bf[:, s, t, b * P:(b + 1) * P, 1],
                                                 dx[:, j, :], start=False, stop=False, skip_group_check=True)
                            pe.wait_ge(lo_ready, base + k + 2)
                            for b in range(GB):
                                w_hi = edge_hi[:, k % NH, b * P:(b + 1) * P]
                                w_lo = edge_lo[:, k % NH, b * P:(b + 1) * P]
                                first = nc.tensor.matmul(psum[:, b, DC:AC], w_hi, xsplit[:, j, 0:D + 1],
                                                         start=False, stop=False, skip_group_check=True)
                                if t == CJ - 1 and b == 0:
                                    first.then_inc(chunk_free, 1)
                                nc.tensor.matmul(psum[:, b, DC:DC + D], w_hi, xsplit[:, j, D + 1:2 * D + 1],
                                                 start=False, stop=False, skip_group_check=True)
                                last = nc.tensor.matmul(psum[:, b, DC:AC], w_lo, xsplit[:, j, 0:D + 1],
                                                        start=False, stop=False, skip_group_check=True)
                            last.then_inc(split_free, 1)
                for b in range(GB):
                    last = sweep(b, AC, False)
                last.then_inc(acc_ready, 1)

        @block.vector
        def _(dve):
            v = nc.vector

            def link(ins, count):
                ins.then_inc(dve_chain, 1)
                dve.wait_ge(dve_chain, count)

            def per_tile(ap):
                return ap.unsqueeze(2).broadcast_to([P, GB, D])

            def all_tiles(ap):
                return ap.unsqueeze(1).broadcast_to([P, GB, D])

            v.memset(V[:, :, 3 * WC], 1.0)
            dve.wait_ge(w_in, 16)
            dve.wait_ge(a_in, 16)
            link(v.tensor_tensor(ta[:, 0, :], Wx[:, 0:D], a_bc[:], ALU.mult), 1)
            v.tensor_reduce(Wx[:, D:WC], ta[:, 0, :].rearrange("p (h d) -> p h d", h=H), AX_X,
                            ALU.add).then_inc(wx_ready, 1)
            dve.wait_ge(ab_in, 32)
            link(v.tensor_scalar(neg_beta, beta_t, -1.0, None, ALU.mult), 2)
            v.tensor_scalar(beta_scale, beta_t, 1.0 / (SPLIT * SPLIT), None, ALU.mult)
            v.tensor_tensor(neg_abs, beta_t, neg_beta, ALU.min).then_inc(scal_ready, 1)
            with dve.Fori(0, NQ // 2) as q2:
                for b in range(2):
                    q = q2 * 2 + b
                    dve.wait_ge(h_ps, q + 2)
                    h_quad = psum[:, 2 + 2 * b:4 + 2 * b, :].rearrange("p k (t c) -> p (k t) c", c=256)
                    v.tensor_copy(G[:, bass.ds(q * QT, QT), :], h_quad[:, :, 0:WC]).then_inc(h_sb, 1)
            dve.wait_ge(h_sb, NQ)
            v.tensor_reduce(smax, G[:, :, D:WC].rearrange("p t h -> p h t"), AX_X, ALU.max).then_inc(smax_ready, 1)
            dve.wait_ge(gmax_ready, 1)
            v.tensor_scalar(negmax, gmax, -1.0, None, ALU.mult).then_inc(negmax_ready, 1)
            dve.wait_ge(e_ready, H)

            def times_e(k):
                tiles = slice(k * CYC, (k + 1) * CYC)
                h_view = G[:, tiles, 0:D].rearrange("p t (h d) -> p t h d", h=H)
                v.tensor_tensor(h_view, h_view, G[:, tiles, D:WC].unsqueeze(3).broadcast_to([P, CYC, H, DH]),
                                ALU.mult).then_inc(eh_ready, 1)

            times_e(0)
            for k in range(TURNS):
                tiles = slice(k * CYC, (k + 1) * CYC)
                if k + 1 < TURNS:
                    times_e(k + 1)
                dve.wait_ge(part_hi, k + 1)
                v.tensor_tensor(G[:, tiles, :], G[:, tiles, :], V[:, tiles, 0:WC], ALU.subtract).then_inc(rest1, 1)
                dve.wait_ge(part_mid, k + 1)
                v.tensor_tensor(V[:, tiles, 2 * WC:3 * WC], G[:, tiles, :], V[:, tiles, WC:2 * WC],
                                ALU.subtract).then_inc(table_ready, 1)
            dve.wait_ge(table_ready, TURNS)
            v.memset(xsplit[:, :, D], 1.0)
            dve.wait_ge(scal_exp, 2)
            link(v.tensor_scalar(sig, sig, 1.0, None, ALU.add), 3)
            link(v.reciprocal(sig, sig), 4)
            v.tensor_scalar(sig_s, sig, 1.0 / SPLIT, None, ALU.mult)
            v.tensor_scalar(neg_sig, sig, -1.0, None, ALU.mult)
            link(v.tensor_scalar(n_c0, c0, float(N), None, ALU.mult), 5)
            FIRST = 5

            def centre(y, c):
                link(v.tensor_reduce(mean, y, AX_X, ALU.add), c + 1)
                link(v.tensor_scalar(mean, mean, -1.0 / D, None, ALU.mult), c + 2)
                link(v.tensor_tensor(ta[:], y, per_tile(mean), ALU.add), c + 3)
                link(v.tensor_tensor(tb[:], ta[:], ta[:], ALU.mult), c + 4)
                link(v.tensor_reduce(ss, tb[:], AX_X, ALU.add), c + 5)
                v.tensor_scalar(var, ss, 1.0 / D, LN_EPS, ALU.mult, ALU.add).then_inc(var_ready, 1)

            dve.wait_ge(bias_in, 16)
            LINKS0 = 13
            with dve.Fori(0, NG // 2) as g2:
                for half in range(2):
                    g = g2 * 2 + half
                    tiles = bass.ds(g * GB, GB)
                    c = dve.snap(g * LINKS0 + FIRST)
                    sums = psum[:, half * GB:(half + 1) * GB, :]
                    dve.wait_ge(sums_ready, g + 1)
                    link(v.tensor_reduce(u[:], sums[:, :, 0:3 * WC].rearrange("p b (k c) -> p b c k", k=3), AX_X,
                                         ALU.add), c + 1)
                    v.tensor_scalar(deg[:, tiles], sums[:, :, 3 * WC], 1.0, None, ALU.max).then_inc(sums_free, 1)
                    link(v.reciprocal(rden[:], u[:, :, D:WC]), c + 2)
                    for h in range(H):
                        ins = v.tensor_tensor(ta[:, :, h * DH:(h + 1) * DH], u[:, :, h * DH:(h + 1) * DH],
                                              rden[:, :, h].unsqueeze(2).broadcast_to([P, GB, DH]), ALU.mult)
                    link(ins, c + 3)
                    link(v.tensor_tensor(ta[:], ta[:], all_tiles(bias_bc[:]), ALU.add), c + 4)
                    v.tensor_scalar(tb[:], ta[:], 0.0, None, ALU.min).then_inc(elu_in, 1)
                    link(v.scalar_tensor_tensor(out=tc[:], in0=ta[:], scalar=0.0, in1=nodes[:, tiles, :],
                                                op0=ALU.max, op1=ALU.add), c + 5)
                    dve.wait_ge(elu_exp, g + 1)
                    link(v.scalar_tensor_tensor(out=tc[:], in0=tb[:], scalar=-1.0, in1=tc[:],
                                                op0=ALU.add, op1=ALU.add), c + 6)
                    centre(tc[:], c + 6)
                    dve.wait_ge(rstd_ready, g + 1)
                    v.tensor_tensor(nodes[:, tiles, :], ta[:], per_tile(rstd), ALU.mult).then_inc(x1_ready, 1)
                    link(v.tensor_tensor(nn, ss, rstd, ALU.mult), c + 12)
                    v.tensor_tensor(nn, nn, rstd, ALU.mult).then_inc(norm_in, 1)
                    dve.wait_ge(norm_pow, g + 1)
                    link(v.tensor_scalar(rnorm[:, tiles], rnorm[:, tiles], 1.0 / NORM_FLOOR, None, ALU.min), c + 13)
                    dve.wait_ge(x1_hi, g + 1)
                    v.scalar_tensor_tensor(out=xsplit[:, tiles, D + 1:2 * D + 1], in0=nodes[:, tiles, :], scalar=SPLIT,
                                           in1=xsplit[:, tiles, 0:D], op0=ALU.mult,
                                           op1=ALU.subtract).then_inc(x1_lo, 1)
            dve.wait_ge(x1_lo, NG)
            dve.sem_inc(all_norms, 1)
            dve.wait_ge(dis_ready, NG)
            with dve.Fori(0, NQ // 2) as q2:
                dve.wait_ge(dx_ready, q2 * 2 + 1)
                for b in range(2):
                    q = q2 * 2 + b
                    tiles = bass.ds(q * QT, QT)
                    v.tensor_tensor(dx_f[b][:], nodes[:, tiles, :],
                                    dis[:, tiles].unsqueeze(2).broadcast_to([P, QT, D]), ALU.mult).then_inc(dx_f32, 1)
                for b in range(2):
                    q = q2 * 2 + b
                    tiles = bass.ds(q * QT, QT)
                    cols = bass.ds(q * QT * P, QT * P)
                    dve.wait_ge(dx_hi_ready, q + 1)
                    v.scalar_tensor_tensor(out=dx[:, tiles, D:DC], in0=dx_f[b][:], scalar=SPLIT, in1=dx[:, tiles, 0:D],
                                           op0=ALU.mult, op1=ALU.subtract).then_inc(dx_ready, 1)
                    dve.wait_ge(unit_hi_ready, q + 1)
                    v.scalar_tensor_tensor(out=unit_lo[:, cols], in0=psum[:, GB + b, :], scalar=SPLIT,
                                           in1=unit_hi[:, cols], op0=ALU.mult,
                                           op1=ALU.subtract).then_inc(unit_ready, 1)
            dve.wait_ge(total_ps, 1)
            v.tensor_scalar(total_bc[:], psum[:, 0, 0:D], c0, None, ALU.mult).then_inc(total_read, 1)
            dve.wait_ge(total_read, 1)
            dve.wait_ge(unit_ready, NQ + 1)
            dve.sem_inc(u_free, 1)
            SECOND = FIRST + NG * LINKS0
            LINKS1 = 12
            with dve.Fori(0, NG) as g:
                with dve.Fori(0, TURNS) as turn:
                    base = dve.snap((g * TURNS + turn) * CYC)

                    def masked(k):
                        if k % CJ == 0:
                            dve.wait_ge(chunk_in[k // CJ], (g * TURNS + turn + NG * TURNS + 1) * 16)
                        if k == 0 or k >= NE:
                            dve.wait_ge(lo_ready, base + max(k - NE + 1, 0) + 1)
                        dve.wait_ge(score_exp, base + k + 1)
                        v.scalar_tensor_tensor(out=edge[:, k % NE, :], in0=psum[:, GB + k % SB, :], scalar=c0,
                                               in1=ring[:, k // CJ, k % CJ, :], op0=ALU.subtract,
                                               op1=ALU.mult).then_inc(edge_ready, 1)

                    masked(0)
                    for k in range(CYC):
                        if k + 1 < CYC:
                            masked(k + 1)
                        dve.wait_ge(hi_ready, base + k + 1)
                        v.tensor_tensor(edge_lo[:, k % NH, :], edge[:, k % NE, :], edge_hi[:, k % NH, :],
                                        ALU.subtract).then_inc(lo_ready, 1)
                c = dve.snap(g * LINKS1 + SECOND)
                tiles = bass.ds(g * GB, GB)
                dve.wait_ge(acc_ready, g + 1)
                v.tensor_reduce(ta[:], acc[:, :, 0:DC].rearrange("p b (k c) -> p b c k", k=2), AX_X,
                                ALU.add).then_inc(diff_summed, 1)
                dve.wait_ge(att_copied, g + 2)
                link(v.tensor_scalar(nn, u[:, :, D], n_c0, None, ALU.add), c + 1)
                link(v.reciprocal(nn, nn), c + 2)
                v.tensor_scalar(mean, dis[:, tiles], 1.0 / SPLIT, None, ALU.mult)
                link(v.tensor_scalar(nn, nn, sig_s, None, ALU.mult), c + 3)
                dve.wait_ge(row_free, g + 1)
                v.tensor_tensor(tb[:], u[:, :, 0:D], all_tiles(total_bc[:]), ALU.add).then_inc(u_free, 1)
                dve.wait_ge(u_free, g + 2)
                link(v.tensor_tensor(tb[:], tb[:], per_tile(nn), ALU.mult), c + 4)
                dve.wait_ge(diff_summed, g + 2)
                link(v.tensor_tensor(ta[:], ta[:], per_tile(mean), ALU.mult), c + 5)
                link(v.tensor_tensor(ta[:], ta[:], tb[:], ALU.add), c + 6)
                link(v.scalar_tensor_tensor(out=tc[:], in0=nodes[:, tiles, :], scalar=neg_sig, in1=ta[:],
                                            op0=ALU.mult, op1=ALU.add), c + 7)
                centre(tc[:], c + 7)
                dve.wait_ge(rstd_ready, g + NG + 1)
                v.tensor_tensor(tb[:], ta[:], per_tile(rstd), ALU.mult).then_inc(out_ready, 1)


_INS = ['x', 'adj', 'L0_gnn_W', 'L0_gnn_a_self', 'L0_gnn_a_neigh', 'L0_gnn_bias', 'L1_gnn_t', 'L1_gnn_alpha',
        'L1_gnn_beta']


def kernel(**inputs):
    import numpy as _np
    import concourse.bacc as _bacc
    from concourse import mybir as _mybir
    from concourse.bass_utils import run_bass_kernel_spmd as _run

    nc = _bacc.Bacc("TRN2", target_bir_lowering=False, num_devices=1)
    arrays, args = {}, []
    for name in _INS:
        a = _np.ascontiguousarray(inputs[name])
        if a.size == 1:
            a = a.reshape(1, 1)
        arrays[f"in_{name}_dram"] = a
        args.append(nc.dram_tensor(f"in_{name}_dram", a.shape, _mybir.dt.from_np(a.dtype), kind="ExternalInput").ap())
    out = nc.dram_tensor("out_0_dram", inputs["x"].shape, F32, kind="ExternalOutput").ap()
    graph_layers_kernel(nc, *args, out)
    r = _run(nc, [arrays], core_ids=[0])
    return r.results[0]["out_0_dram"]
```

```python
from contextlib import ExitStack

import concourse.bass as bass
from concourse import mybir
from concourse.alu_op_type import AluOpType as ALU

ACT = mybir.ActivationFunctionType
F32 = mybir.dt.float32
F16 = mybir.dt.float16
I32 = mybir.dt.int32
U32 = mybir.dt.uint32
BF16 = mybir.dt.bfloat16
AX_X = mybir.AxisListType.X
RMAX = bass.bass_isa.ReduceOp.max

P = 128
LN_EPS = 1e-5
NORM_FLOOR = 1e-8

SPLIT = 4096.0


def graph_layers_kernel(nc, x, adj, W, a_self, a_neigh, bias, t_in, alpha, beta, out):
    N, D = x.shape
    H, _, DH = W.shape
    NT = N // P
    GB = 4
    GW = GB * P
    NG = N // GW
    CJ = 4
    RING = 4
    CYC = CJ * RING
    TURNS = NT // CYC
    WC = D + H
    VC = 3 * WC + 1
    XC = 2 * D + 2
    DC = 2 * D
    AC = DC + D + 1
    AHEAD = 3
    SB = 4
    NE = 4
    NH = 4
    QT = 4
    NQ = NT // QT
    BITS = 16
    WPT = P // BITS
    NW = NT * WPT
    LEVELS = 3
    SLOTS = 16
    SELF = SLOTS
    ROW = D + 2
    STEPS = (8, 10, 12, SLOTS)
    NGB = 2 * QT
    DQ = 4
    NDQ = 4
    LINKS0 = 52
    LINKS1 = 12
    LINKS_A, LINKS_B = 17, 8
    assert NW <= 512 and NGB * (NT // NGB) == NT
    assert D == P and H * DH == D and NG * GW == N and TURNS * CYC == NT and NG % 2 == 0

    adj_chunks = adj.rearrange("(c t p) (g w) -> g c p t w", t=CJ, p=P, w=GW)
    scratch = nc.dram_tensor("scratch_rows", (N, ROW), F32, kind="Internal").ap()
    scratch_groups = scratch.rearrange("(g b p) f -> g p b f", b=GB, p=P)
    x_quarters = x.rearrange("(k t p) f -> k p t f", k=4, p=P)
    out_groups = out.rearrange("(g b p) f -> g p b f", b=GB, p=P)

    with ExitStack() as ctx:
        def sb(name, shape, dt):
            return ctx.enter_context(nc.sbuf_tensor(name, shape, dt))

        def sem(name):
            return ctx.enter_context(nc.semaphore(name))

        psum = ctx.enter_context(nc.psum_tensor("psum", [P, 8, 512], F32))

        ring = sb("ring", [P, RING, CJ, GW], F32)
        ring_bf = ring[:].bitcast(BF16).rearrange("p r t (w e) -> p r t w e", e=2)
        nodes = sb("nodes", [P, NT, ROW], F32)
        rnorm, dis = nodes[:, :, D], nodes[:, :, D + 1]
        TABLE = NT * (VC + 1) // 2
        arena = sb("arena", [P, TABLE + N], F32)
        V = arena[:, 0:TABLE].bitcast(BF16).rearrange("p (t c) -> p t c", c=VC + 1)
        dx = arena[:, 0:NT * D].bitcast(F16).rearrange("p (t c) -> p t c", c=DC)
        unit_hi = arena[:, TABLE:TABLE + N // 2].bitcast(F16)
        unit_lo = arena[:, TABLE + N // 2:TABLE + N].bitcast(F16)
        LISTS = NGB * SLOTS * ROW
        rows = arena[:, 0:LISTS].rearrange("p (b s c) -> p b s c", b=NGB, s=SLOTS)
        at = [LISTS]

        def carve(n, dt=F32):
            at[0] += n
            assert LISTS >= TABLE and at[0] <= TABLE + N
            piece = arena[:, at[0] - n:at[0]]
            return piece if dt == F32 else piece.bitcast(dt)

        keys = carve(NT * SLOTS).rearrange("p (t s) -> p t s", s=SLOTS)
        is_slot = carve(NT * (SLOTS + 1)).rearrange("p (t s) -> p t s", s=SLOTS + 1)
        index = carve(NT * SLOTS, U32).rearrange("p (t s) -> p t s", s=SLOTS)
        w_val = carve(GB * SLOTS)
        w_at = carve(GB * SLOTS, U32)
        w_base = carve(GB * SLOTS)
        w_exp = carve(GB * SLOTS, I32)
        w_top = carve(GB * SLOTS, I32)
        found = carve(GB * LEVELS * SLOTS)
        wide = sb("wide", [P, NT * WC], F32)
        G = wide[:].rearrange("p (t c) -> p t c", c=WC)
        xsplit = wide[:].bitcast(F16)[:, 0:NT * XC].rearrange("p (t c) -> p t c", c=XC)
        PROD = SLOTS * D
        prod = [wide[:, i * PROD:(i + 1) * PROD].rearrange("p (s d) -> p s d", d=D) for i in range(2)]
        DIAG = DQ * P
        diag = [wide[:, 2 * PROD + i * DIAG:2 * PROD + (i + 1) * DIAG].rearrange("p (s d) -> p s d", d=P)
                for i in range(NDQ)]
        rest = 2 * PROD + NDQ * DIAG
        SL = QT * (SLOTS + 1)
        cosine, weight, hop, coef0, coef1 = (wide[:, rest + i * SL:rest + (i + 1) * SL].rearrange(
            "p (t s) -> p t s", s=SLOTS + 1) for i in range(5))
        coef = (coef0, coef1)
        ones32 = wide[:, rest + 5 * SL:rest + 5 * SL + P]
        edge = sb("edge", [P, NE, GW], F32)
        edge_hi = sb("edge_hi", [P, NH, GW], F16)
        edge_lo = sb("edge_lo", [P, NH, GW], F16)
        words = edge
        xT = edge
        ta = sb("ta", [P, GB, D], F32)
        tb = sb("tb", [P, GB, D], F32)
        tc = sb("tc", [P, GB, D], F32)
        u = sb("u", [P, GB, WC], F32)
        key_q = tc[:, 0, 0:GB * SLOTS]
        u_flat = u[:].rearrange("p b c -> p (b c)")
        index_q = u_flat[:, 0:2 * QT * SLOTS].bitcast(U32).rearrange("p (h c) -> p h c", h=2)
        quotient = u_flat[:, 2 * QT * SLOTS:2 * QT * SLOTS + 2 * QT].rearrange("p (h c) -> p h c", h=2)
        ident = sb("ident", [P, P], F32)
        Wx = sb("Wx", [P, WC], F32)
        zeros = sb("zeros", [P, VC + 1], BF16)
        ones16 = sb("ones16", [P, P], F16)
        bias_bc = sb("bias_bc", [P, D], F32)
        total_bc = sb("total_bc", [P, D], F32)
        a_bc = bias_bc
        deg = sb("deg", [P, NT], F32)
        norm2 = sb("norm2", [P, NT], F32)
        node_id = sb("node_id", [P, NT], F32)
        bits = sb("bits", [P, WPT], BF16)
        counts = sb("counts", [P, NT + 1], F32)
        most = sb("most", [P, NT + 1], F32)
        steps = sb("steps", [P, NT + 1], I32)
        due = sb("due", [P, NT], F32)
        due_i = sb("due_i", [P, NT], I32)
        degree = sb("degree", [P, NT], F32)
        node_q = sb("node_q", [P, GB], F32)
        sm = sb("sm", [P, 40], F32)
        shorts = sm[:, 38:39]
        smax, negmax = sm[:, 0:H], sm[:, 2:2 + H]
        alpha_t, beta_t = sm[:, 4:5], sm[:, 5:6]
        neg_beta, neg_abs, c0 = sm[:, 6:7], sm[:, 7:8], sm[:, 8:9]
        beta_scale, sig, neg_sig, n_c0, sig_s = sm[:, 9:10], sm[:, 10:11], sm[:, 11:12], sm[:, 12:13], sm[:, 13:14]
        mean, ss, var, rstd, nn = (sm[:, 16 + 4 * i:20 + 4 * i] for i in range(5))
        gmax = sm[:, 36:36 + H]
        dx_f = (ta, tb)
        unit_f = (tc[:], u[:, :, 0:D])
        rden = sb("rden", [P, GB, H], F32)
        mhalf = sb("mhalf", [P, GB], F32)

        x_in = [sem(f"x_in{k}") for k in range(4)]
        w_in = sem("w_in")
        a_in = sem("a_in")
        bias_in = sem("bias_in")
        ab_in = sem("ab_in")
        chunk_in = [sem(f"chunk_in{s}") for s in range(RING)]
        chunk_free = sem("chunk_free")
        consts = sem("consts")
        ids_ready = sem("ids_ready")
        wx_ready = sem("wx_ready")
        xT_ps = sem("xT_ps")
        xT_sb = sem("xT_sb")
        h_ps = sem("h_ps")
        h_sb = sem("h_sb")
        smax_ready = sem("smax_ready")
        gmax_ready = sem("gmax_ready")
        negmax_ready = sem("negmax_ready")
        e_ready = sem("e_ready")
        eh_ready = sem("eh_ready")
        part_hi = sem("part_hi")
        rest1 = sem("rest1")
        part_mid = sem("part_mid")
        table_ready = sem("table_ready")
        scal_ready = sem("scal_ready")
        scal_exp = sem("scal_exp")
        sums_ready = sem("sums_ready")
        sums_free = sem("sums_free")
        elu_in = sem("elu_in")
        elu_exp = sem("elu_exp")
        var_ready = sem("var_ready")
        rstd_ready = sem("rstd_ready")
        norm_in = sem("norm_in")
        norm_pow = sem("norm_pow")
        x1_ready = sem("x1_ready")
        words_ready = sem("words_ready")
        words_free = sem("words_free")
        words_sb = sem("words_sb")
        words_used = sem("words_used")
        rows_ready = sem("rows_ready")
        rows_stored = sem("rows_stored")
        x1_hi = sem("x1_hi")
        x1_lo = sem("x1_lo")
        all_norms = sem("all_norms")
        unit_f32 = sem("unit_f32")
        unit_ps = sem("unit_ps")
        unit_hi_ready = sem("unit_hi_ready")
        unit_ready = sem("unit_ready")
        dx_f32 = sem("dx_f32")
        dx_hi_ready = sem("dx_hi_ready")
        dx_ready = sem("dx_ready")
        total_ps = sem("total_ps")
        total_read = sem("total_read")
        score_ps = sem("score_ps")
        score_exp = sem("score_exp")
        edge_ready = sem("edge_ready")
        hi_ready = sem("hi_ready")
        lo_ready = sem("lo_ready")
        split_free = sem("split_free")
        acc_ready = sem("acc_ready")
        diff_summed = sem("diff_summed")
        u_free = sem("u_free")
        att_copied = sem("att_copied")
        out_ready = sem("out_ready")
        stored = sem("stored")
        row_free = sem("row_free")
        dis_ready = sem("dis_ready")
        dve_chain = sem("dve_chain")
        dve_chain1 = sem("dve_chain1")
        wait_carrier = sem("wait_carrier")
        counted = sem("counted")
        counts_max = sem("counts_max")
        chosen = sem("chosen")
        gather_start = sem("gather_start")
        gathered = [sem(f"gathered{i}") for i in range(NGB)]
        index_ready = sem("index_ready")
        index_used = sem("index_used")
        cos_ready = sem("cos_ready")
        cos_exp = sem("cos_exp")
        coef_ready = sem("coef_ready")
        diag_ready = sem("diag_ready")
        diag_used = sem("diag_used")
        tile_done = sem("tile_done")
        total32_ps = sem("total32_ps")
        total32_read = sem("total32_read")
        near_read = sem("near_read")
        g_var = sem("g_var")
        g_rstd = sem("g_rstd")
        g_out = sem("g_out")
        g_stored = sem("g_stored")
        g_out_free = sem("g_out_free")

        acc = psum[:, 0:GB, :]

        block = ctx.enter_context(nc.Block())

        @block.sync
        def _(sp):
            sp.dma_start(Wx[:, 0:D].rearrange("p (h d) -> p h d", h=H),
                         W.rearrange("h f d -> f h d")).then_inc(w_in, 16)
            sp.dma_start(a_bc[:], a_neigh.rearrange("h d -> (h d)").partition_broadcast(P)).then_inc(a_in, 16)
            sp.dma_start(alpha_t, alpha.rearrange("a b -> (a b)").partition_broadcast(P)).then_inc(ab_in, 16)
            sp.dma_start(beta_t, beta.rearrange("a b -> (a b)").partition_broadcast(P)).then_inc(ab_in, 16)
            for k in range(4):
                sp.dma_start(nodes[:, k * (NT // 4):(k + 1) * (NT // 4), 0:D], x_quarters[k]).then_inc(x_in[k], 16)
            sp.wait_ge(wx_ready, 1)
            sp.dma_start(bias_bc[:], bias.partition_broadcast(P)).then_inc(bias_in, 16)
            def load_chunks(layer):
                with sp.Fori(0, NG) as g:
                    with sp.Fori(0, TURNS) as turn:
                        for s in range(RING):
                            sp.wait_ge(chunk_free, layer * NG * TURNS * RING + (g * TURNS + turn) * RING + s + 1)
                            sp.dma_start(ring[:, s], adj_chunks[g, turn * RING + s]).then_inc(chunk_in[s], 16)

            load_chunks(0)
            sp.wait_ge(chosen, 1)
            dense = sp.value_load(steps[0:1, NT:NT + 1], min_val=0, max_val=1)
            with sp.If(dense > 0):
                load_chunks(1)
            with sp.Else():
                with sp.Fori(0, NQ) as q:
                    sp.wait_ge(g_out, q + 1)
                    sp.dma_start(out_groups[q], tb[:]).then_inc(g_stored, 16)
                    sp.wait_ge(g_stored, q * 16 + 16)
                    sp.sem_inc(g_out_free, 1)
            sp.nop()

        @block.gpsimd
        def _(pool):
            pool.memset(mhalf[:], -0.5).then_inc(consts, 1)
            pool.memset(ones16[:], 1.0).then_inc(consts, 1)
            pool.memset(zeros[:], 0.0).then_inc(consts, 1)
            pool.memset(ident[:], 0.0).then_inc(consts, 1)
            pool.wait_ge(consts, 4)
            pool.affine_select(out=ident[:], in_=ident[:], compare_op=ALU.not_equal, fill=1.0, base=0,
                               pattern=[[-1, P]], channel_multiplier=1).then_inc(consts, 1)
            pool.memset(bits[:], 0.0).then_inc(consts, 1)
            for r in range(BITS):
                pool.wait_ge(consts, 6 + r)
                pool.affine_select(out=bits[:], in_=bits[:], compare_op=ALU.not_equal, fill=float(2 ** r), base=-r,
                                   pattern=[[-BITS, WPT]], channel_multiplier=1).then_inc(consts, 1)
            pool.iota(due_i[:], pattern=[[P, NT]], base=1, channel_multiplier=1).then_inc(ids_ready, 1)
            pool.wait_ge(smax_ready, 1)
            pool.partition_all_reduce(gmax, smax, P, RMAX).then_inc(gmax_ready, 1)
            with pool.Fori(0, NG) as g:
                tiles = bass.ds(g * GB, GB)
                pool.wait_ge(var_ready, g + 1)
                pool.tensor_tensor(rstd, var, mhalf[:, 0:GB], ALU.pow).then_inc(rstd_ready, 1)
                pool.tensor_tensor(dis[:, tiles], deg[:, tiles], mhalf[:, 0:GB], ALU.pow).then_inc(dis_ready, 1)
                pool.wait_ge(norm_in, g + 1)
                pool.tensor_tensor(rnorm[:, tiles], norm2[:, tiles], mhalf[:, 0:GB], ALU.pow).then_inc(norm_pow, 1)
            pool.wait_ge(counted, 1)
            pool.partition_all_reduce(most[:], counts[:], P, RMAX).then_inc(counts_max, 1)
            pool.wait_ge(rows_stored, 16 * NG)
            pool.wait_ge(chosen, 1)
            dense = pool.value_load(steps[0:1, NT:NT + 1], min_val=0, max_val=1)

            with pool.If(dense > 0):
                with pool.Fori(0, NQ // 2) as q2:
                    for b in range(2):
                        tiles = bass.ds((q2 * 2 + b) * QT, QT)
                        pool.wait_ge(unit_ps, q2 * 2 + 1)
                        pool.tensor_tensor(unit_f[b], nodes[:, tiles, 0:D],
                                           rnorm[:, tiles].unsqueeze(2).broadcast_to([P, QT, D]),
                                           ALU.mult).then_inc(unit_f32, 1)
                with pool.Fori(0, NG) as g:
                    pool.wait_ge(var_ready, g + NG + 1)
                    pool.tensor_tensor(rstd, var, mhalf[:, 0:GB], ALU.pow).then_inc(rstd_ready, 1)
                    pool.wait_ge(out_ready, g + 1)
                    pool.dma_start(out_groups[g], tb[:]).then_inc(stored, 16)
                    pool.wait_ge(stored, g * 16 + 16)
                    pool.sem_inc(row_free, 1)
                pool.wait_ge(stored, 16 * NG)
            with pool.Else():
                def gather(q, half):
                    pool.wait_ge(index_ready, q + 1)
                    for b in range(QT):
                        def take(s):
                            c = b * SLOTS + s
                            pool.indirect_dma_start(
                                rows[:, half * QT + b, s, :], None, scratch,
                                bass.IndirectOffsetOnAxis(ap=index_q[:, half, c:c + 1], axis=0),
                                bounds_check=N - 1, oob_is_err=False).then_inc(gathered[half * QT + b], 16)

                        taken = pool.value_load(steps[0:1, bass.ds(q * QT + b, 1)], min_val=STEPS[0], max_val=SLOTS)
                        for s in range(STEPS[0]):
                            take(s)
                        for lo, hi in zip(STEPS, STEPS[1:]):
                            with pool.If(taken > lo):
                                for s in range(lo, hi):
                                    take(s)
                        pool.nop()

                def near_pow(q):
                    pool.wait_ge(g_var, q + 1)
                    pool.tensor_tensor(rstd, var, mhalf[:, 0:GB], ALU.pow).then_inc(g_rstd, 1)

                pool.wait_ge(gather_start, 1)
                gather(0, 0)
                gather(1, 1)
                with pool.Fori(0, NQ // 2 - 1) as q2:
                    for half in range(2):
                        pool.wait_ge(diag_used, (q2 * 2 + half + 1) * QT * SLOTS // DQ + NDQ)
                        gather(q2 * 2 + half + 2, half)
                        near_pow(q2 * 2 + half)
                near_pow(NQ - 2)
                near_pow(NQ - 1)
            pool.nop()

        @block.scalar
        def _(act):
            with act.Fori(0, NQ // 2) as q2:
                act.wait_ge(h_ps, q2 * 2 + 1)
                for b in range(2):
                    act.wait_ge(xT_ps, q2 * 2 + b + 1)
                    act.activation(xT[:, b, :], psum[:, b, :], ACT.Copy).then_inc(xT_sb, 1)
            act.wait_ge(scal_ready, 1)
            act.activation(c0, neg_abs, ACT.Exp).then_inc(scal_exp, 1)
            act.activation(sig, alpha_t, ACT.Exp, scale=-1.0).then_inc(scal_exp, 1)
            act.wait_ge(negmax_ready, 1)
            for h in range(H):
                act.activation(G[:, :, D + h], G[:, :, D + h], ACT.Exp, bias=negmax[:, h:h + 1]).then_inc(e_ready, 1)
            for k in range(TURNS):
                tiles = slice(k * CYC, (k + 1) * CYC)
                act.wait_ge(eh_ready, k + 1)
                act.activation(V[:, tiles, 0:WC], G[:, tiles, :], ACT.Copy).then_inc(part_hi, 1)
                act.wait_ge(rest1, k + 1)
                act.activation(V[:, tiles, WC:2 * WC], G[:, tiles, :], ACT.Copy).then_inc(part_mid, 1)
            with act.Fori(0, NG) as g:
                tiles = bass.ds(g * GB, GB)
                act.wait_ge(sums_ready, g + 1)
                act.wait_ge(words_used, g + 1)
                for b in range(GB):
                    act.activation(words[:, b, 0:NW], psum[:, GB + b, 0:NW], ACT.Copy).then_inc(words_free, 1)
                act.wait_ge(elu_in, g + 1)
                act.activation(tb[:], tb[:], ACT.Exp).then_inc(elu_exp, 1)
                act.wait_ge(rows_ready, g + 1)
                act.dma_start(scratch_groups[g], nodes[:, tiles, :]).then_inc(rows_stored, 16)
            act.wait_ge(chosen, 1)
            dense = act.value_load(steps[0:1, NT:NT + 1], min_val=0, max_val=1)

            def exp_scores(bank, n):
                act.wait_ge(score_ps, n + 1)
                act.activation(psum[:, GB + bank, :], psum[:, GB + bank, :], ACT.Exp, bias=neg_abs,
                               scale=beta_scale).then_inc(score_exp, 1)

            with act.If(dense > 0):
                with act.Fori(0, NQ) as q:
                    tiles = bass.ds(q * QT, QT)
                    act.activation(xsplit[:, tiles, 0:D], nodes[:, tiles, 0:D], ACT.Copy,
                                   scale=SPLIT).then_inc(x1_hi, 1)
                with act.Fori(0, NQ // 2) as q2:
                    for b in range(2):
                        q = q2 * 2 + b
                        act.wait_ge(dx_f32, q + 1)
                        act.activation(dx[:, bass.ds(q * QT, QT), 0:D], dx_f[b][:], ACT.Copy,
                                       scale=SPLIT).then_inc(dx_hi_ready, 1)
                        act.wait_ge(unit_ps, q + 2)
                        act.activation(unit_hi[:, bass.ds(q * QT * P, QT * P)], psum[:, GB + b, :], ACT.Copy,
                                       scale=SPLIT).then_inc(unit_hi_ready, 1)
                exp_scores(0, 0)
                with act.Fori(0, NG) as g:
                    with act.Fori(0, TURNS) as turn:
                        base = act.snap((g * TURNS + turn) * CYC)
                        for k in range(CYC):
                            exp_scores((k + 1) % SB, base + k + 1)
                            act.wait_ge(edge_ready, base + k + 2)
                            act.wait_ge(split_free, base + k + 1)
                            act.activation(edge_hi[:, k % NH, :], edge[:, k % NE, :], ACT.Copy).then_inc(hi_ready, 1)
                    act.wait_ge(diff_summed, g + 2)
                    act.wait_ge(u_free, g + 1)
                    act.activation(u[:, :, 0:D + 1], acc[:, :, DC:AC], ACT.Copy).then_inc(att_copied, 1)
            with act.Else():
                def near_weights(q, half):
                    act.wait_ge(cos_ready, q + 1)
                    act.activation(weight, cosine, ACT.Exp, bias=neg_abs, scale=beta_t).then_inc(cos_exp, 1)
                    act.wait_ge(coef_ready, q + 1)
                    for d in range(QT * SLOTS // DQ):
                        act.wait_ge(diag_used, q * (QT * SLOTS // DQ) + d + 1)
                        b, s = divmod(d * DQ, SLOTS)
                        for k in range(DQ):
                            last = act.activation(diag[d % NDQ][:, k, :], ident[:], ACT.Copy,
                                                  scale=coef[half][:, b, s + k:s + k + 1])
                        last.then_inc(diag_ready, 1)

                with act.Fori(0, NQ // 2) as q2:
                    for half in range(2):
                        near_weights(q2 * 2 + half, half)
            act.nop()

        @block.tensor
        def _(pe):
            pe.sem_inc(chunk_free, RING)
            pe.sem_inc(sums_free, GB)
            pe.sem_inc(words_free, GB)
            pe.sem_inc(diag_used, NDQ)
            pe.sem_inc(near_read, 2)
            pe.sem_inc(split_free, NH)
            for start in (h_ps, unit_ps, unit_ready, dx_ready, diff_summed, att_copied, edge_ready, lo_ready, row_free,
                          words_used, g_out_free):
                pe.sem_inc(start, 1)
            pe.wait_ge(consts, 6 + BITS)
            pe.wait_ge(wx_ready, 1)
            for q2 in range(NQ // 2):
                pe.wait_ge(x_in[q2 // 2], 16)
                for b in range(2):
                    for t in range(QT):
                        last = nc.tensor.transpose(psum[:, b, t * P:(t + 1) * P], nodes[:, (q2 * 2 + b) * QT + t, 0:D],
                                                   ident[:])
                    last.then_inc(xT_ps, 1)
                if q2:
                    pe.wait_ge(h_sb, q2 * 2)
                for b in range(2):
                    pe.wait_ge(xT_sb, q2 * 2 + b + 1)
                    for t in range(QT):
                        c = (t % 2) * 256
                        last = nc.tensor.matmul(psum[:, 2 + 2 * b + t // 2, c:c + WC],
                                                xT[:, b, t * P:(t + 1) * P], Wx[:], start=True, stop=True)
                    last.then_inc(h_ps, 1)
            pe.wait_ge(h_sb, NQ)

            def sweep(bank, cols, first):
                return nc.tensor.matmul(psum[:, bank, 0:cols], zeros[:, 0:P], zeros[:, 0:cols],
                                        start=first, stop=not first, skip_group_check=True)

            def neighbour_sums(g, turn, first):
                pe.wait_ge(table_ready, turn + 1)
                for s in range(RING):
                    pe.wait_ge(chunk_in[s], (g * TURNS + turn + 1) * 16)
                    for b in range(GB):
                        if first and s == 0:
                            pe.wait_ge(sums_free, g * GB + b + 1)
                            pe.wait_ge(words_free, g * GB + b + 1)
                        for t in range(CJ):
                            adj_ji = ring_bf[:, s, t, b * P:(b + 1) * P, 1]
                            nc.tensor.matmul(psum[:, b, 0:VC], adj_ji, V[:, turn * CYC + s * CJ + t, 0:VC],
                                             start=first and s == 0 and t == 0, stop=False, skip_group_check=True)
                            last = nc.tensor.matmul(psum[:, GB + b, bass.ds((turn * CYC + s * CJ + t) * WPT, WPT)],
                                                    adj_ji, bits[:], start=True, stop=True, skip_group_check=True)
                    last.then_inc(chunk_free, 1)

            with pe.Fori(0, NG) as g:
                neighbour_sums(g, 0, True)
                with pe.Fori(1, TURNS) as turn:
                    neighbour_sums(g, turn, False)
                for b in range(GB):
                    last = sweep(b, VC, False)
                last.then_inc(sums_ready, 1)
            pe.wait_ge(chosen, 1)
            dense = pe.value_load(steps[0:1, NT:NT + 1], min_val=0, max_val=1)
            with pe.If(dense > 0):
                pe.wait_ge(x1_lo, NG)
                pe.wait_ge(sums_free, NG * GB + GB)
                sweep(0, D, True)
                with pe.Fori(0, NQ) as q:
                    for t in range(QT):
                        for part in (0, D + 1):
                            nc.tensor.matmul(psum[:, 0, 0:D], ones16[:], xsplit[:, q * QT + t, part:part + D],
                                             start=False, stop=False, skip_group_check=True)
                sweep(0, D, False).then_inc(total_ps, 1)
                with pe.Fori(0, NQ // 2) as q2:
                    pe.wait_ge(unit_ready, q2 * 2 + 1)
                    for b in range(2):
                        pe.wait_ge(unit_f32, q2 * 2 + b + 1)
                        for t in range(QT):
                            last = nc.tensor.transpose(psum[:, GB + b, t * P:(t + 1) * P], unit_f[b][:, t, :], ident[:])
                        last.then_inc(unit_ps, 1)
                pe.wait_ge(unit_ready, NQ + 1)
                pe.wait_ge(dx_ready, NQ + 1)
                pe.wait_ge(total_read, 1)

                def scores(bank, tile, group):
                    hi_j, lo_j = (part[:, bass.ds(tile * P, P)] for part in (unit_hi, unit_lo))
                    hi_i, lo_i = (part[:, bass.ds(group * GW, GW)] for part in (unit_hi, unit_lo))
                    nc.tensor.matmul(psum[:, GB + bank, :], hi_j, hi_i, start=True, stop=False)
                    nc.tensor.matmul(psum[:, GB + bank, :], hi_j, lo_i, start=False, stop=False)
                    nc.tensor.matmul(psum[:, GB + bank, :], lo_j, hi_i, start=False, stop=True).then_inc(score_ps, 1)

                for n in range(AHEAD):
                    scores(n, n, 0)
                with pe.Fori(0, NG) as g:
                    pe.wait_ge(diff_summed, g + 1)
                    pe.wait_ge(att_copied, g + 1)
                    for b in range(GB):
                        sweep(b, AC, True)
                    with pe.Fori(0, TURNS) as turn:
                        base = pe.snap((g * TURNS + turn) * CYC)
                        next_turn = pe.snap((turn + 1) % TURNS)
                        next_group = pe.snap((g + (turn + 1) // TURNS) % NG)
                        for s in range(RING):
                            pe.wait_ge(chunk_in[s], (g * TURNS + turn + NG * TURNS + 1) * 16)
                            for t in range(CJ):
                                k = s * CJ + t
                                pe.wait_ge(edge_ready, base + k + 1)
                                if k + AHEAD < CYC:
                                    scores((k + AHEAD) % SB, turn * CYC + k + AHEAD, g)
                                else:
                                    scores((k + AHEAD) % SB, next_turn * CYC + k + AHEAD - CYC, next_group)
                                j = turn * CYC + k
                                for b in range(GB):
                                    nc.tensor.matmul(psum[:, b, 0:DC], ring_bf[:, s, t, b * P:(b + 1) * P, 1],
                                                     dx[:, j, :], start=False, stop=False, skip_group_check=True)
                                pe.wait_ge(lo_ready, base + k + 2)
                                for b in range(GB):
                                    w_hi = edge_hi[:, k % NH, b * P:(b + 1) * P]
                                    w_lo = edge_lo[:, k % NH, b * P:(b + 1) * P]
                                    first = nc.tensor.matmul(psum[:, b, DC:AC], w_hi, xsplit[:, j, 0:D + 1],
                                                             start=False, stop=False, skip_group_check=True)
                                    if t == CJ - 1 and b == 0:
                                        first.then_inc(chunk_free, 1)
                                    nc.tensor.matmul(psum[:, b, DC:DC + D], w_hi, xsplit[:, j, D + 1:2 * D + 1],
                                                     start=False, stop=False, skip_group_check=True)
                                    last = nc.tensor.matmul(psum[:, b, DC:AC], w_lo, xsplit[:, j, 0:D + 1],
                                                            start=False, stop=False, skip_group_check=True)
                                last.then_inc(split_free, 1)
                    for b in range(GB):
                        last = sweep(b, AC, False)
                    last.then_inc(acc_ready, 1)
            with pe.Else():
                pe.wait_ge(gather_start, 1)
                sweep(7, D, True)
                with pe.Fori(0, NQ) as q:
                    for t in range(QT):
                        nc.tensor.matmul(psum[:, 7, 0:D], ones32, nodes[:, q * QT + t, 0:D],
                                         start=False, stop=False, skip_group_check=True)
                sweep(7, D, False).then_inc(total32_ps, 1)
                pe.wait_ge(total32_read, 1)
                with pe.Fori(0, NQ // 2) as q2:
                    for half in range(2):
                        q = q2 * 2 + half
                        pe.wait_ge(near_read, q + 1)
                        for d in range(QT * SLOTS // DQ):
                            b, s = divmod(d * DQ, SLOTS)
                            pe.wait_ge(diag_ready, q * (QT * SLOTS // DQ) + d + 1)
                            for k in range(DQ):
                                last = nc.tensor.matmul(psum[:, half * QT + b, 0:D], diag[d % NDQ][:, k, :],
                                                        rows[:, half * QT + b, s + k, 0:D],
                                                        start=s + k == 0, stop=s + k == SLOTS - 1)
                            last.then_inc(diag_used, 1)
            pe.nop()

        @block.vector
        def _(dve):
            v = nc.vector

            class Chain:
                def __init__(self, sem):
                    self.sem, self.base, self.n = sem, 0, 0

                def start(self, base):
                    self.base, self.n = base, 0

                def __call__(self, ins, settle=False):
                    self.n += 1
                    ins.then_inc(self.sem, 1)
                    dve.wait_ge(self.sem, self.base + self.n)
                    if settle:
                        settled()

            def settled():
                dve.sem_inc(wait_carrier, 1)

            link = Chain(dve_chain)

            def per_tile(ap):
                return ap.unsqueeze(2).broadcast_to([P, GB, D])

            def all_tiles(ap):
                return ap.unsqueeze(1).broadcast_to([P, GB, D])

            v.memset(V[:, :, 3 * WC], 1.0)
            dve.wait_ge(ids_ready, 1)
            v.tensor_copy(node_id[:], due_i[:])
            dve.wait_ge(w_in, 16)
            dve.wait_ge(a_in, 16)
            link(v.tensor_tensor(ta[:, 0, :], Wx[:, 0:D], a_bc[:], ALU.mult))
            v.tensor_reduce(Wx[:, D:WC], ta[:, 0, :].rearrange("p (h d) -> p h d", h=H), AX_X,
                            ALU.add).then_inc(wx_ready, 1)
            dve.wait_ge(ab_in, 32)
            link(v.tensor_scalar(neg_beta, beta_t, -1.0, None, ALU.mult))
            v.tensor_scalar(beta_scale, beta_t, 1.0 / (SPLIT * SPLIT), None, ALU.mult)
            v.tensor_tensor(neg_abs, beta_t, neg_beta, ALU.min).then_inc(scal_ready, 1)
            with dve.Fori(0, NQ // 2) as q2:
                for b in range(2):
                    q = q2 * 2 + b
                    dve.wait_ge(h_ps, q + 2)
                    h_quad = psum[:, 2 + 2 * b:4 + 2 * b, :].rearrange("p k (t c) -> p (k t) c", c=256)
                    v.tensor_copy(G[:, bass.ds(q * QT, QT), :], h_quad[:, :, 0:WC]).then_inc(h_sb, 1)
            dve.wait_ge(h_sb, NQ)
            v.tensor_reduce(smax, G[:, :, D:WC].rearrange("p t h -> p h t"), AX_X, ALU.max).then_inc(smax_ready, 1)
            dve.wait_ge(gmax_ready, 1)
            v.tensor_scalar(negmax, gmax, -1.0, None, ALU.mult).then_inc(negmax_ready, 1)
            dve.wait_ge(e_ready, H)

            def times_e(k):
                tiles = slice(k * CYC, (k + 1) * CYC)
                h_view = G[:, tiles, 0:D].rearrange("p t (h d) -> p t h d", h=H)
                v.tensor_tensor(h_view, h_view, G[:, tiles, D:WC].unsqueeze(3).broadcast_to([P, CYC, H, DH]),
                                ALU.mult).then_inc(eh_ready, 1)

            times_e(0)
            for k in range(TURNS):
                tiles = slice(k * CYC, (k + 1) * CYC)
                if k + 1 < TURNS:
                    times_e(k + 1)
                dve.wait_ge(part_hi, k + 1)
                v.tensor_tensor(G[:, tiles, :], G[:, tiles, :], V[:, tiles, 0:WC], ALU.subtract).then_inc(rest1, 1)
                dve.wait_ge(part_mid, k + 1)
                v.tensor_tensor(V[:, tiles, 2 * WC:3 * WC], G[:, tiles, :], V[:, tiles, WC:2 * WC],
                                ALU.subtract).then_inc(table_ready, 1)
            dve.wait_ge(scal_exp, 2)
            link(v.tensor_scalar(sig, sig, 1.0, None, ALU.add))
            link(v.reciprocal(sig, sig))
            v.tensor_scalar(sig_s, sig, 1.0 / SPLIT, None, ALU.mult)
            v.tensor_scalar(neg_sig, sig, -1.0, None, ALU.mult)
            link(v.tensor_scalar(n_c0, c0, float(N), None, ALU.mult))

            FIRST = link.n

            def centre(y, link, done):
                link(v.tensor_reduce(mean, y, AX_X, ALU.add))
                link(v.tensor_scalar(mean, mean, -1.0 / D, None, ALU.mult))
                link(v.tensor_tensor(ta[:], y, per_tile(mean), ALU.add))
                link(v.tensor_tensor(tb[:], ta[:], ta[:], ALU.mult))
                link(v.tensor_reduce(ss, tb[:], AX_X, ALU.add))
                v.tensor_scalar(var, ss, 1.0 / D, LN_EPS, ALU.mult, ALU.add).then_inc(done, 1)

            def quotient_and_norm(g, tiles):
                dve.wait_ge(sums_ready, g + 1)
                v.tensor_scalar(counts_deg(tiles), psum[:, 0:GB, 3 * WC], 1.0, None, ALU.mult)
                for b in range(GB):
                    v.tensor_reduce(u[:, b, :], psum[:, b, 0:3 * WC].rearrange("p (k c) -> p c k", k=3), AX_X,
                                    ALU.add).then_inc(sums_free, 1)
                dve.wait_ge(sums_free, (g + 2) * GB)
                link(v.reciprocal(rden[:], u[:, :, D:WC]))
                for h in range(H):
                    ins = v.tensor_tensor(ta[:, :, h * DH:(h + 1) * DH], u[:, :, h * DH:(h + 1) * DH],
                                          rden[:, :, h].unsqueeze(2).broadcast_to([P, GB, DH]), ALU.mult)
                link(ins)
                link(v.tensor_tensor(ta[:], ta[:], all_tiles(bias_bc[:]), ALU.add))
                v.tensor_scalar(tb[:], ta[:], 0.0, None, ALU.min).then_inc(elu_in, 1)
                v.tensor_scalar(deg[:, tiles], counts_deg(tiles), 1.0, None, ALU.max)
                link(v.scalar_tensor_tensor(out=tc[:], in0=ta[:], scalar=0.0, in1=nodes[:, tiles, 0:D],
                                            op0=ALU.max, op1=ALU.add))
                dve.wait_ge(elu_exp, g + 1)
                link(v.scalar_tensor_tensor(out=tc[:], in0=tb[:], scalar=-1.0, in1=tc[:],
                                            op0=ALU.add, op1=ALU.add))
                centre(tc[:], link, var_ready)
                dve.wait_ge(rstd_ready, g + 1)
                v.tensor_tensor(nodes[:, tiles, 0:D], ta[:], per_tile(rstd), ALU.mult)
                link(v.tensor_tensor(nn, ss, rstd, ALU.mult))
                v.tensor_tensor(norm2[:, tiles], nn, rstd, ALU.mult).then_inc(norm_in, 1)

            def list_neighbours(g, tiles):
                dve.wait_ge(words_free, (g + 2) * GB)
                settled()
                for b in range(GB):
                    row, lo, hi = words[:, b, 0:NW], b * SLOTS, b * SLOTS + 8
                    link(v.max(out=w_val[:, lo:lo + 8], in_=row), settle=True)
                    v.max_index(out=w_at[:, lo:lo + 8], in_max=w_val[:, lo:lo + 8], in_values=row)
                    link(v.match_replace(out=row, in_to_replace=w_val[:, lo:lo + 8], in_values=row, imm_value=0.0), settle=True)
                    link(v.max(out=w_val[:, hi:hi + 8], in_=row), settle=True)
                    ins = v.max_index(out=w_at[:, hi:hi + 8], in_max=w_val[:, hi:hi + 8], in_values=row)
                ins.then_inc(words_used, 1)
                dve.wait_ge(words_used, g + 2)
                link(v.tensor_scalar(w_base, w_at, float(BITS), None, ALU.mult))
                by_level = found.rearrange("p (b l s) -> p b l s", l=LEVELS, s=SLOTS)
                for level in range(LEVELS):
                    v.tensor_scalar(w_exp, w_val.bitcast(I32), 23, None, ALU.logical_shift_right)
                    link(v.tensor_scalar(w_top, w_val.bitcast(I32), 0x7F800000, None, ALU.bitwise_and))
                    key = by_level[:, :, level, :]
                    four = lambda ap: ap.rearrange("p (b s) -> p b s", s=SLOTS)
                    link(v.scalar_tensor_tensor(out=key, in0=four(w_exp), scalar=-126.0, in1=four(w_base),
                                                op0=ALU.add, op1=ALU.add))
                    link(v.scalar_tensor_tensor(out=key, in0=four(w_val), scalar=0.0, in1=key, op0=ALU.is_gt,
                                                op1=ALU.mult))
                    link(v.tensor_tensor(w_val, w_val, w_top.bitcast(F32), ALU.subtract))
                for b in range(GB):
                    part = found[:, b * LEVELS * SLOTS:(b + 1) * LEVELS * SLOTS]
                    link(v.scalar_tensor_tensor(out=part, in0=part, scalar=node_q[:, b:b + 1], in1=part,
                                                op0=ALU.not_equal, op1=ALU.mult), settle=True)
                for b in range(GB):
                    part = found[:, b * LEVELS * SLOTS:(b + 1) * LEVELS * SLOTS]
                    lo, hi = b * SLOTS, b * SLOTS + 8
                    link(v.max(out=key_q[:, lo:lo + 8], in_=part), settle=True)
                    link(v.match_replace(out=part, in_to_replace=key_q[:, lo:lo + 8], in_values=part, imm_value=0.0), settle=True)
                    ins = v.max(out=key_q[:, hi:hi + 8], in_=part)
                link(ins)
                kq = key_q.rearrange("p (b s) -> p b s", s=SLOTS)
                link(v.tensor_scalar(is_slot[:, tiles, 0:SLOTS], kq, 0.0, None, ALU.is_gt))
                v.tensor_reduce(counts[:, tiles], is_slot[:, tiles, 0:SLOTS], AX_X, ALU.add)
                ids = node_q[:].unsqueeze(2).broadcast_to([P, GB, SLOTS])
                wb = w_base.rearrange("p (b s) -> p b s", s=SLOTS)
                link(v.tensor_tensor(wb, is_slot[:, tiles, 0:SLOTS], ids, ALU.mult))
                link(v.tensor_tensor(wb, ids, wb, ALU.subtract))
                v.scalar_tensor_tensor(out=index[:, tiles, :], in0=wb, scalar=-1.0, in1=kq, op0=ALU.add, op1=ALU.add)

            def counts_deg(tiles):
                return degree[:, tiles]

            def dense_layer():
                v.memset(xsplit[:, :, D], 1.0)
                with dve.Fori(0, NQ) as q:
                    tiles = bass.ds(q * QT, QT)
                    dve.wait_ge(x1_hi, q + 1)
                    v.scalar_tensor_tensor(out=xsplit[:, tiles, D + 1:2 * D + 1], in0=nodes[:, tiles, 0:D], scalar=SPLIT,
                                           in1=xsplit[:, tiles, 0:D], op0=ALU.mult,
                                           op1=ALU.subtract).then_inc(x1_lo, 1)
                with dve.Fori(0, NQ // 2) as q2:
                    dve.wait_ge(dx_ready, q2 * 2 + 1)
                    for b in range(2):
                        q = q2 * 2 + b
                        tiles = bass.ds(q * QT, QT)
                        v.tensor_tensor(dx_f[b][:], nodes[:, tiles, 0:D],
                                        dis[:, tiles].unsqueeze(2).broadcast_to([P, QT, D]), ALU.mult).then_inc(dx_f32, 1)
                    for b in range(2):
                        q = q2 * 2 + b
                        tiles = bass.ds(q * QT, QT)
                        cols = bass.ds(q * QT * P, QT * P)
                        dve.wait_ge(dx_hi_ready, q + 1)
                        v.scalar_tensor_tensor(out=dx[:, tiles, D:DC], in0=dx_f[b][:], scalar=SPLIT, in1=dx[:, tiles, 0:D],
                                               op0=ALU.mult, op1=ALU.subtract).then_inc(dx_ready, 1)
                        dve.wait_ge(unit_hi_ready, q + 1)
                        v.scalar_tensor_tensor(out=unit_lo[:, cols], in0=psum[:, GB + b, :], scalar=SPLIT,
                                               in1=unit_hi[:, cols], op0=ALU.mult,
                                               op1=ALU.subtract).then_inc(unit_ready, 1)
                dve.wait_ge(total_ps, 1)
                v.tensor_scalar(total_bc[:], psum[:, 0, 0:D], c0, None, ALU.mult).then_inc(total_read, 1)
                dve.wait_ge(total_read, 1)
                dve.wait_ge(unit_ready, NQ + 1)
                dve.sem_inc(u_free, 1)
                link1 = Chain(dve_chain1)
                with dve.Fori(0, NG) as g:
                    with dve.Fori(0, TURNS) as turn:
                        base = dve.snap((g * TURNS + turn) * CYC)

                        def masked(k):
                            if k % CJ == 0:
                                dve.wait_ge(chunk_in[k // CJ], (g * TURNS + turn + NG * TURNS + 1) * 16)
                            if k == 0 or k >= NE:
                                dve.wait_ge(lo_ready, base + max(k - NE + 1, 0) + 1)
                            dve.wait_ge(score_exp, base + k + 1)
                            v.scalar_tensor_tensor(out=edge[:, k % NE, :], in0=psum[:, GB + k % SB, :], scalar=c0,
                                                   in1=ring[:, k // CJ, k % CJ, :], op0=ALU.subtract,
                                                   op1=ALU.mult).then_inc(edge_ready, 1)

                        masked(0)
                        for k in range(CYC):
                            if k + 1 < CYC:
                                masked(k + 1)
                            dve.wait_ge(hi_ready, base + k + 1)
                            v.tensor_tensor(edge_lo[:, k % NH, :], edge[:, k % NE, :], edge_hi[:, k % NH, :],
                                            ALU.subtract).then_inc(lo_ready, 1)
                    link1.start(dve.snap(g * LINKS1))
                    tiles = bass.ds(g * GB, GB)
                    dve.wait_ge(acc_ready, g + 1)
                    v.tensor_reduce(ta[:], acc[:, :, 0:DC].rearrange("p b (k c) -> p b c k", k=2), AX_X,
                                    ALU.add).then_inc(diff_summed, 1)
                    dve.wait_ge(att_copied, g + 2)
                    link1(v.tensor_scalar(nn, u[:, :, D], n_c0, None, ALU.add))
                    link1(v.reciprocal(nn, nn))
                    v.tensor_scalar(mean, dis[:, tiles], 1.0 / SPLIT, None, ALU.mult)
                    link1(v.tensor_scalar(nn, nn, sig_s, None, ALU.mult))
                    dve.wait_ge(row_free, g + 1)
                    v.tensor_tensor(tb[:], u[:, :, 0:D], all_tiles(total_bc[:]), ALU.add).then_inc(u_free, 1)
                    dve.wait_ge(u_free, g + 2)
                    link1(v.tensor_tensor(tb[:], tb[:], per_tile(nn), ALU.mult))
                    dve.wait_ge(diff_summed, g + 2)
                    link1(v.tensor_tensor(ta[:], ta[:], per_tile(mean), ALU.mult))
                    link1(v.tensor_tensor(ta[:], ta[:], tb[:], ALU.add))
                    link1(v.scalar_tensor_tensor(out=tc[:], in0=nodes[:, tiles, 0:D], scalar=neg_sig, in1=ta[:],
                                                op0=ALU.mult, op1=ALU.add))
                    centre(tc[:], link1, var_ready)
                    dve.wait_ge(rstd_ready, g + NG + 1)
                    v.tensor_tensor(tb[:], ta[:], per_tile(rstd), ALU.mult).then_inc(out_ready, 1)
                    assert link1.n == LINKS1, link1.n

            def gathered_layer():
                v.memset(rows[:, :, STEPS[0]:, :], 0.0)
                v.memset(ones32, 1.0).then_inc(gather_start, 1)
                near = Chain(dve_chain1)

                def next_index(q, half):
                    v.tensor_copy(index_q[:, half, :].rearrange("p (b s) -> p b s", s=SLOTS),
                                  index[:, bass.ds(q * QT, QT), :]).then_inc(index_ready, 1)

                def coefficients(q, half, base):
                    near.start(base)
                    tiles = bass.ds(q * QT, QT)
                    bufs = slice(half * QT, (half + 1) * QT)
                    c17 = coef[half]
                    for b in range(QT):
                        reach = dve.value_load(due_i[0:1, bass.ds(q * QT + b, 1)], min_val=16 * STEPS[0],
                                               max_val=16 * SLOTS * NT // NGB)
                        dve.wait_ge(gathered[half * QT + b], reach)
                        near(v.tensor_tensor(prod[b % 2], rows[:, half * QT + b, :, 0:D],
                                             nodes[:, q * QT + b, 0:D].unsqueeze(1).broadcast_to([P, SLOTS, D]),
                                             ALU.mult))
                        ins = v.tensor_reduce(cosine[:, b, 0:SLOTS], prod[b % 2], AX_X, ALU.add)
                    near(ins)
                    near(v.tensor_tensor(cosine[:, :, 0:SLOTS], cosine[:, :, 0:SLOTS], rows[:, bufs, :, D], ALU.mult))
                    near(v.tensor_tensor(cosine[:, :, SELF], norm2[:, tiles], rnorm[:, tiles], ALU.mult))
                    v.tensor_tensor(cosine, cosine, per_slot(rnorm[:, tiles]), ALU.mult).then_inc(cos_ready, 1)
                    near(v.tensor_tensor(hop[:, :, 0:SLOTS], rows[:, bufs, :, D + 1], is_slot[:, tiles, 0:SLOTS],
                                         ALU.mult))
                    near(v.tensor_scalar(hop[:, :, SELF], dis[:, tiles], 1.0, None, ALU.mult))
                    near(v.tensor_tensor(hop, hop, per_slot(dis[:, tiles]), ALU.mult))
                    dve.wait_ge(cos_exp, q + 1)
                    near(v.scalar_tensor_tensor(out=weight, in0=weight, scalar=c0, in1=is_slot[:, tiles, :],
                                                op0=ALU.subtract, op1=ALU.mult))
                    share = quotient[:, half, :]
                    near(v.tensor_reduce(share, weight, AX_X, ALU.add))
                    near(v.tensor_scalar(share, share, n_c0, None, ALU.add))
                    near(v.reciprocal(share, share))
                    near(v.tensor_scalar(share, share, sig, None, ALU.mult))
                    near(v.tensor_tensor(weight, weight, per_slot(share), ALU.mult))
                    near(v.tensor_tensor(c17, weight, hop, ALU.add))
                    v.tensor_scalar(c17[:, :, SELF], c17[:, :, SELF], sig, None, ALU.subtract).then_inc(coef_ready, 1)
                    assert near.n == LINKS_A, near.n

                def finish(q, half, base):
                    near.start(base)
                    tiles = bass.ds(q * QT, QT)
                    dve.wait_ge(g_out_free, q + 1)
                    near(v.tensor_tensor(ta[:], nodes[:, tiles, 0:D], per_tile(coef[half][:, :, SELF]), ALU.mult))
                    near(v.tensor_tensor(tb[:], all_tiles(total_bc[:]), per_tile(quotient[:, half, :]), ALU.mult))
                    near(v.tensor_tensor(ta[:], ta[:], tb[:], ALU.add))
                    dve.wait_ge(diag_used, q * (QT * SLOTS // DQ) + QT * SLOTS // DQ + NDQ)
                    v.tensor_tensor(tc[:], ta[:], psum[:, half * QT:(half + 1) * QT, 0:D], ALU.add)\
                     .then_inc(near_read, 1)
                    dve.wait_ge(near_read, q + 3)
                    centre(tc[:], near, g_var)
                    dve.wait_ge(g_rstd, q + 1)
                    v.tensor_tensor(tb[:], ta[:], per_tile(rstd), ALU.mult).then_inc(g_out, 1)
                    assert near.n == LINKS_B, near.n

                def per_slot(ap):
                    return ap.unsqueeze(2).broadcast_to([P, QT, SLOTS + 1])

                next_index(0, 0)
                next_index(1, 1)
                dve.wait_ge(total32_ps, 1)
                v.tensor_scalar(total_bc[:], psum[:, 7, 0:D], c0, None, ALU.mult).then_inc(total32_read, 1)
                dve.wait_ge(total32_read, 1)
                LINKS_AB = LINKS_A + LINKS_B
                coefficients(0, 0, 0)
                next_index(2, 0)
                with dve.Fori(0, NQ // 2 - 1) as q2:
                    for half in range(2):
                        q = q2 * 2 + half
                        base = dve.snap(q * LINKS_AB + LINKS_A)
                        coefficients(q + 1, 1 - half, base)
                        next_index((q + 3) % NQ, 1 - half)
                        finish(q, half, base + LINKS_A)
                base = (NQ - 2) * LINKS_AB + LINKS_A
                coefficients(NQ - 1, 1, base)
                finish(NQ - 2, 0, base + LINKS_A)
                finish(NQ - 1, 1, base + LINKS_AB)

            dve.wait_ge(bias_in, 16)
            v.memset(is_slot[:, :, SELF], 1.0)
            with dve.Fori(0, NG) as g:
                tiles = bass.ds(g * GB, GB)
                link.start(dve.snap(g * LINKS0 + FIRST))
                quotient_and_norm(g, tiles)
                v.tensor_copy(node_q[:], node_id[:, tiles])
                dve.wait_ge(norm_pow, g + 1)
                dve.wait_ge(dis_ready, g + 1)
                v.tensor_scalar(rnorm[:, tiles], rnorm[:, tiles], 1.0 / NORM_FLOOR, None,
                                ALU.min).then_inc(rows_ready, 1)
                list_neighbours(g, tiles)
                assert link.n == LINKS0, link.n
            link.start(NG * LINKS0 + FIRST)
            link(v.scalar_tensor_tensor(out=due[:], in0=counts[:, 0:NT], scalar=1.0, in1=degree[:], op0=ALU.add,
                                        op1=ALU.not_equal))
            v.tensor_reduce(counts[:, NT:NT + 1], due[:], AX_X, ALU.max).then_inc(counted, 1)
            dve.wait_ge(counts_max, 1)
            slots, flag = most[:, 0:NT], steps[:, NT:NT + 1]
            link(v.tensor_scalar(due[:], slots, float(STEPS[0]), float(STEPS[1] - STEPS[0]), ALU.is_gt, ALU.mult))
            link(v.tensor_scalar(due[:], due[:], float(STEPS[0]), None, ALU.add))
            for lo, hi, more in zip(STEPS[1:], STEPS[2:], (counts, degree)):
                link(v.tensor_scalar(more[:, 0:NT], slots, float(lo), float(hi - lo), ALU.is_gt, ALU.mult))
                link(v.tensor_tensor(due[:], due[:], more[:, 0:NT], ALU.add))
            v.tensor_copy(steps[:, 0:NT], due[:])
            v.tensor_copy(flag, most[:, NT:NT + 1])
            link(v.tensor_scalar(due[:], due[:], 16.0, None, ALU.mult))
            for t in range(NGB, NT, NGB):
                link(v.tensor_tensor(due[:, t:t + NGB], due[:, t:t + NGB], due[:, t - NGB:t], ALU.add))
            v.tensor_copy(due_i[:], due[:]).then_inc(chosen, 1)
            dve.wait_ge(chosen, 1)
            dense = dve.value_load(steps[0:1, NT:NT + 1], min_val=0, max_val=1)

            with dve.If(dense > 0):
                dense_layer()
            with dve.Else():
                gathered_layer()
            dve.nop()


_INS = ['x', 'adj', 'L0_gnn_W', 'L0_gnn_a_self', 'L0_gnn_a_neigh', 'L0_gnn_bias', 'L1_gnn_t', 'L1_gnn_alpha',
        'L1_gnn_beta']


def kernel(**inputs):
    import numpy as _np
    import concourse.bacc as _bacc
    from concourse import mybir as _mybir
    from concourse.bass_utils import run_bass_kernel_spmd as _run

    nc = _bacc.Bacc("TRN2", target_bir_lowering=False, num_devices=1)
    arrays, args = {}, []
    for name in _INS:
        a = _np.ascontiguousarray(inputs[name])
        if a.size == 1:
            a = a.reshape(1, 1)
        arrays[f"in_{name}_dram"] = a
        args.append(nc.dram_tensor(f"in_{name}_dram", a.shape, _mybir.dt.from_np(a.dtype), kind="ExternalInput").ap())
    out = nc.dram_tensor("out_0_dram", inputs["x"].shape, F32, kind="ExternalOutput").ap()
    graph_layers_kernel(nc, *args, out)
    r = _run(nc, [arrays], core_ids=[0])
    return r.results[0]["out_0_dram"]
```

```python
from contextlib import ExitStack

import concourse.bass as bass
from concourse import mybir
from concourse.alu_op_type import AluOpType as ALU

ACT = mybir.ActivationFunctionType
F32 = mybir.dt.float32
F16 = mybir.dt.float16
I32 = mybir.dt.int32
U32 = mybir.dt.uint32
BF16 = mybir.dt.bfloat16
AX_X = mybir.AxisListType.X

P = 128
LN_EPS = 1e-5
NORM_FLOOR = 1e-8

SPLIT = 4096.0


def graph_layers_kernel(nc, x, adj, W, a_self, a_neigh, bias, t_in, alpha, beta, out):
    N, D = x.shape
    H, _, DH = W.shape
    NT = N // P
    GB = 4
    GW = GB * P
    NG = N // GW
    CJ = 4
    RING0 = 8
    TURNS0 = NT // (CJ * RING0)
    LOADS0 = NG * TURNS0
    RING = 4
    CYC = CJ * RING
    TURNS = NT // CYC
    WC = D + H
    VC = 3 * WC + 1
    XC = 2 * D + 2
    DC = 2 * D
    AC = DC + D + 1
    AHEAD = 3
    SB = 4
    NE = 4
    NH = 4
    QT = 4
    NQ = NT // QT
    BITS = 16
    WPT = P // BITS
    NW = NT * WPT
    LEVELS = 3
    SLOTS = 16
    ROW = D + 2
    OWN_ABS, OWN_IS, OWN_LIST = ROW, ROW + 1, ROW + 2 + SLOTS
    OWN = OWN_LIST + SLOTS
    LISTED = OWN - ROW
    THIRDS = 3
    HELD = 6
    EARLY = NT - GB
    AHEAD_OF_ALL = 2 * SLOTS
    SIZES = (4, 8, SLOTS)
    PARTS = 16
    NDQ = 4
    LINKS0 = 52
    LINKS1 = 12
    LINKS_A, LINKS_B = 17, 8
    assert HELD % THIRDS == 0 and NQ - 2 * HELD == THIRDS + 1 and HELD * QT % 8 == 0
    assert NW <= 512 and (NQ - 1) % THIRDS == 0 and N & (N - 1) == 0
    assert D == P and H * DH == D and NG * GW == N and TURNS * CYC == NT and NG % 2 == 0

    adj_chunks = adj.rearrange("(c t p) (g w) -> g c p t w", t=CJ, p=P, w=GW)
    scratch = nc.dram_tensor("scratch_rows", (N, ROW), F32, kind="Internal").ap()
    scratch_groups = scratch.rearrange("(g b p) f -> g p b f", b=GB, p=P)
    scratch_own = nc.dram_tensor("scratch_own", (N, OWN), F32, kind="Internal").ap()
    own_groups = scratch_own.rearrange("(g b p) f -> g p b f", b=GB, p=P)
    x_quarters = x.rearrange("(k t p) f -> k p t f", k=4, p=P)
    out_groups = out.rearrange("(g b p) f -> g p b f", b=GB, p=P)

    with ExitStack() as ctx:
        def sb(name, shape, dt):
            return ctx.enter_context(nc.sbuf_tensor(name, shape, dt))

        def sem(name):
            return ctx.enter_context(nc.semaphore(name))

        psum = ctx.enter_context(nc.psum_tensor("psum", [P, 8, 512], F32))

        ring = sb("ring", [P, RING, CJ, GW], F32)
        ring_bf = ring[:].bitcast(BF16).rearrange("p r t (w e) -> p r t w e", e=2)
        nodes = sb("nodes", [P, NT, ROW], F32)
        rnorm, dis = nodes[:, :, D], nodes[:, :, D + 1]
        TABLE = NT * (VC + 1) // 2
        arena = sb("arena", [P, TABLE + N], F32)
        more = arena[:, TABLE:TABLE + N].rearrange("p (r t w) -> p r t w", t=CJ, w=GW)
        more_bf = more.bitcast(BF16).rearrange("p r t (w e) -> p r t w e", e=2)
        ring0 = [ring[:, s] for s in range(RING)] + [more[:, s] for s in range(RING0 - RING)]
        ring0_bf = [ring_bf[:, s] for s in range(RING)] + [more_bf[:, s] for s in range(RING0 - RING)]
        V = arena[:, 0:TABLE].bitcast(BF16).rearrange("p (t c) -> p t c", c=VC + 1)
        dx = arena[:, 0:NT * D].bitcast(F16).rearrange("p (t c) -> p t c", c=DC)
        unit_hi = arena[:, TABLE:TABLE + N // 2].bitcast(F16)
        unit_lo = arena[:, TABLE + N // 2:TABLE + N].bitcast(F16)
        QUAD_ROWS = QT * SLOTS * ROW
        rows = [piece.rearrange("p (b s c) -> p b s c", b=QT, s=SLOTS) for piece in
                (arena[:, 0:QUAD_ROWS], arena[:, QUAD_ROWS:2 * QUAD_ROWS], nodes[:].rearrange("p t c -> p (t c)"))]
        listing = sb("edge_hi", [P, NH * GW // 2], F32)
        at = [0]

        def carve(n, dt=F32):
            at[0] += n
            assert at[0] <= NH * GW // 2 and 2 * QUAD_ROWS <= TABLE + N and NT * ROW == QUAD_ROWS
            piece = listing[:, at[0] - n:at[0]]
            return piece if dt == F32 else piece.bitcast(dt)

        lists = carve(GB * LISTED).rearrange("p (t s) -> p t s", s=LISTED)
        is_slot = lists[:, :, 2:2 + SLOTS]
        list_u = lists.bitcast(U32)[:, :, 2 + SLOTS:]
        order = carve(NT)
        order_i = carve(NT, I32)
        node_ix = carve(NT, I32)
        places = carve(NT)
        own_ix = carve(HELD * QT, U32)
        first_steps = carve(QT, I32)
        w_val = carve(GB * SLOTS)
        w_at = carve(GB * SLOTS, U32)
        w_base = carve(GB * SLOTS)
        w_exp = carve(GB * SLOTS, I32)
        w_top = carve(GB * SLOTS, I32)
        found = carve(GB * LEVELS * SLOTS)
        wide = sb("wide", [P, NT * WC], F32)
        G = wide[:].rearrange("p (t c) -> p t c", c=WC)
        xsplit = wide[:].bitcast(F16)[:, 0:NT * XC].rearrange("p (t c) -> p t c", c=XC)
        PROD = SLOTS * D
        ring_flat = ring[:].rearrange("p r t w -> p (r t w)")
        prod = [ring_flat[:, i * PROD:(i + 1) * PROD].rearrange("p (s d) -> p s d", d=D) for i in range(2)]
        DIAG = QT * SLOTS // PARTS * P
        diag = [ring_flat[:, 2 * PROD + i * DIAG:2 * PROD + (i + 1) * DIAG].rearrange("p (s d) -> p s d", d=P)
                for i in range(NDQ)]
        SL = QT * (SLOTS + 1)
        cosine, weight, hop, *coef = (wide[:, i * SL:(i + 1) * SL].rearrange(
            "p (t s) -> p t s", s=SLOTS + 1) for i in range(3 + THIRDS))
        rest = (3 + THIRDS) * SL
        ones32 = wide[:, rest:rest + P]
        rest += P
        own = wide[:, rest:rest + HELD * QT * OWN].rearrange("p (t c) -> p t c", c=OWN)
        edge = sb("edge", [P, NE, GW], F32)
        edge_hi = listing[:].bitcast(F16).rearrange("p (k w) -> p k w", w=GW)
        edge_lo = sb("edge_lo", [P, NH, GW], F16)
        words = edge
        xT = edge
        ta = sb("ta", [P, GB, D], F32)
        tb = sb("tb", [P, GB, D], F32)
        tc = sb("tc", [P, GB, D], F32)
        u = sb("u", [P, GB, WC], F32)
        key_q = tc[:, 0, 0:GB * SLOTS]
        result = [edge[:, i, :].rearrange("p (b d) -> p b d", d=D) for i in range(THIRDS)]
        u_flat = u[:].rearrange("p b c -> p (b c)")
        store_ix = u_flat[:, 0:THIRDS * QT].bitcast(U32).rearrange("p (h c) -> p h c", h=THIRDS)
        quotient = u_flat[:, THIRDS * QT:2 * THIRDS * QT].rearrange("p (h c) -> p h c", h=THIRDS)
        ident = sb("ident", [P, P], F32)
        Wx = sb("Wx", [P, WC], F32)
        zeros = sb("zeros", [P, VC + 1], BF16)
        ones16 = sb("ones16", [P, P], F16)
        bias_bc = sb("bias_bc", [P, D], F32)
        total_bc = sb("total_bc", [P, D], F32)
        a_bc = bias_bc
        deg = sb("deg", [P, NT], F32)
        norm2 = sb("norm2", [P, NT], F32)
        node_id = sb("node_id", [P, NT], F32)
        bits = sb("bits", [P, WPT], BF16)
        counts = sb("counts", [P, NT], F32)
        longest = sb("longest", [P, NT + 1], F32)
        most = psum[:, 7, 0:NT + 1]
        steps = sb("steps", [P, NT + 1], I32)
        due = sb("due", [P, NT], F32)
        due_i = sb("due_i", [P, NT], I32)
        degree = sb("degree", [P, NT], F32)
        node_q = sb("node_q", [P, GB], F32)
        sm = sb("sm", [P, 40], F32)
        peak = sm[:, 38:39]
        smax, negmax = sm[:, 0:H], sm[:, 2:2 + H]
        alpha_t, beta_t = sm[:, 4:5], sm[:, 5:6]
        neg_beta, neg_abs, c0 = sm[:, 6:7], sm[:, 7:8], sm[:, 8:9]
        beta_scale, sig, neg_sig, n_c0, sig_s = sm[:, 9:10], sm[:, 10:11], sm[:, 11:12], sm[:, 12:13], sm[:, 13:14]
        mean, ss, var, rstd, nn = (sm[:, 16 + 4 * i:20 + 4 * i] for i in range(5))
        ones_k = ta[:, 1, :]
        peaks = tb[:, 0, :]
        dx_f = (ta, tb)
        unit_f = (tc[:], u[:, :, 0:D])
        rden = sb("rden", [P, GB, H], F32)
        mhalf = sb("mhalf", [P, GB], F32)

        x_in = [sem(f"x_in{k}") for k in range(4)]
        w_in = sem("w_in")
        a_in = sem("a_in")
        bias_in = sem("bias_in")
        ab_in = sem("ab_in")
        chunk_in = [sem(f"chunk_in{s}") for s in range(RING0)]
        chunk_free = sem("chunk_free")
        consts = sem("consts")
        ids_ready = sem("ids_ready")
        wx_ready = sem("wx_ready")
        xT_ps = sem("xT_ps")
        xT_sb = sem("xT_sb")
        h_ps = sem("h_ps")
        h_sb = sem("h_sb")
        smax_ready = sem("smax_ready")
        smax_turned = sem("smax_turned")
        peaks_ready = sem("peaks_ready")
        counts_turned = sem("counts_turned")
        gmax_ready = sem("gmax_ready")
        negmax_ready = sem("negmax_ready")
        e_ready = sem("e_ready")
        eh_ready = sem("eh_ready")
        part_hi = sem("part_hi")
        rest1 = sem("rest1")
        part_mid = sem("part_mid")
        table_ready = sem("table_ready")
        scal_ready = sem("scal_ready")
        scal_exp = sem("scal_exp")
        sums_ready = sem("sums_ready")
        sums_free = sem("sums_free")
        elu_in = sem("elu_in")
        elu_exp = sem("elu_exp")
        var_ready = sem("var_ready")
        rstd_ready = sem("rstd_ready")
        norm_in = sem("norm_in")
        norm_pow = sem("norm_pow")
        words_free = sem("words_free")
        words_used = sem("words_used")
        rows_ready = sem("rows_ready")
        rows_stored = sem("rows_stored")
        lists_ready = sem("lists_ready")
        lists_stored = sem("lists_stored")
        x1_hi = sem("x1_hi")
        x1_lo = sem("x1_lo")
        unit_f32 = sem("unit_f32")
        unit_ps = sem("unit_ps")
        unit_hi_ready = sem("unit_hi_ready")
        unit_ready = sem("unit_ready")
        dx_f32 = sem("dx_f32")
        dx_hi_ready = sem("dx_hi_ready")
        dx_ready = sem("dx_ready")
        total_ps = sem("total_ps")
        total_read = sem("total_read")
        score_ps = sem("score_ps")
        score_exp = sem("score_exp")
        edge_ready = sem("edge_ready")
        hi_ready = sem("hi_ready")
        lo_ready = sem("lo_ready")
        split_free = sem("split_free")
        acc_ready = sem("acc_ready")
        diff_summed = sem("diff_summed")
        u_free = sem("u_free")
        att_copied = sem("att_copied")
        out_ready = sem("out_ready")
        stored = sem("stored")
        row_free = sem("row_free")
        dis_ready = sem("dis_ready")
        dve_chain = sem("dve_chain")
        dve_chain1 = sem("dve_chain1")
        wait_carrier = sem("wait_carrier")
        pool_wait_carrier = sem("pool_wait_carrier")
        counted = sem("counted")
        counts_max = sem("counts_max")
        chosen = sem("chosen")
        gathered = [sem(f"gathered{i}") for i in range(THIRDS)]
        own_in = [sem(f"own_in{i}") for i in range(HELD)]
        rows_clear = sem("rows_clear")
        last_rows_stored = sem("last_rows_stored")
        last_lists_stored = sem("last_lists_stored")
        first_counted = sem("first_counted")
        first_max = sem("first_max")
        first_turned = sem("first_turned")
        first_ready = sem("first_ready")
        first_done = sem("first_done")
        own_ix_ready = sem("own_ix_ready")
        cos_ready = sem("cos_ready")
        cos_exp = sem("cos_exp")
        coef_ready = sem("coef_ready")
        diag_ready = sem("diag_ready")
        diag_used = sem("diag_used")
        total32_ps = sem("total32_ps")
        total32_read = sem("total32_read")
        near_read = sem("near_read")
        g_var = sem("g_var")
        g_rstd = sem("g_rstd")
        g_out = sem("g_out")
        g_stored = [sem(f"g_stored{i}") for i in range(THIRDS)]
        g_out_free = sem("g_out_free")

        acc = psum[:, 0:GB, :]

        def by_size(engine, q, quad):
            taken = engine.value_load(steps[0:1, bass.ds(q * QT, 1)], min_val=1, max_val=SLOTS)

            def choose(sizes):
                if len(sizes) == 1:
                    quad(sizes[0])
                else:
                    with engine.If(taken > sizes[0]):
                        choose(sizes[1:])
                    with engine.Else():
                        quad(sizes[0])

            choose(SIZES)
            engine.nop()

        block = ctx.enter_context(nc.Block())

        @block.sync
        def _(sp):
            def load_x(k):
                sp.dma_start(nodes[:, k * (NT // 4):(k + 1) * (NT // 4), 0:D], x_quarters[k]).then_inc(x_in[k], 16)

            load_x(0)
            sp.dma_start(Wx[:, 0:D].rearrange("p (h d) -> p h d", h=H),
                         W.rearrange("h f d -> f h d")).then_inc(w_in, 16)
            sp.dma_start(a_bc[:], a_neigh.rearrange("h d -> (h d)").partition_broadcast(P)).then_inc(a_in, 16)
            sp.dma_start(alpha_t, alpha.rearrange("a b -> (a b)").partition_broadcast(P)).then_inc(ab_in, 16)
            sp.dma_start(beta_t, beta.rearrange("a b -> (a b)").partition_broadcast(P)).then_inc(ab_in, 16)
            for k in range(1, 4):
                load_x(k)
            sp.wait_ge(wx_ready, 1)
            sp.dma_start(bias_bc[:], bias.partition_broadcast(P)).then_inc(bias_in, 16)

            def load_chunks(slots, turns, freed):
                with sp.Fori(0, NG) as g:
                    with sp.Fori(0, turns) as turn:
                        for s, slot in enumerate(slots):
                            sp.wait_ge(chunk_free, (g * turns + turn) * len(slots) + s + freed)
                            sp.dma_start(slot, adj_chunks[g, turn * len(slots) + s]).then_inc(chunk_in[s], 16)

            load_chunks(ring0, TURNS0, 1)
            sp.wait_ge(chosen, 1)
            dense = sp.value_load(steps[0:1, NT:NT + 1], min_val=0, max_val=1)
            with sp.If(dense > 0):
                sp.wait_ge(first_done, 1)
                load_chunks([ring[:, s] for s in range(RING)], TURNS, LOADS0 * RING0 + RING0 - RING + 1)
            with sp.Else():
                with sp.Fori(0, NQ // THIRDS) as q3:
                    for third in range(THIRDS):
                        sp.wait_ge(g_stored[third], (q3 + 1) * QT * 16)
                        sp.sem_inc(g_out_free, 1)
                sp.wait_ge(g_stored[0], (NQ // THIRDS + 1) * QT * 16)
                sp.sem_inc(g_out_free, 1)
            sp.nop()

        @block.gpsimd
        def _(pool):
            pool.memset(mhalf[:], -0.5).then_inc(consts, 1)
            pool.memset(ones16[:], 1.0).then_inc(consts, 1)
            pool.memset(zeros[:], 0.0).then_inc(consts, 1)
            pool.memset(ident[:], 0.0).then_inc(consts, 1)
            pool.wait_ge(consts, 4)
            pool.affine_select(out=ident[:], in_=ident[:], compare_op=ALU.not_equal, fill=1.0, base=0,
                               pattern=[[-1, P]], channel_multiplier=1).then_inc(consts, 1)
            pool.memset(bits[:], 0.0).then_inc(consts, 1)
            for r in range(BITS):
                pool.wait_ge(consts, 6 + r)
                pool.affine_select(out=bits[:], in_=bits[:], compare_op=ALU.not_equal, fill=float(2 ** r), base=-r,
                                   pattern=[[-BITS, WPT]], channel_multiplier=1).then_inc(consts, 1)
            pool.iota(due_i[:], pattern=[[P, NT]], base=1, channel_multiplier=1).then_inc(ids_ready, 1)
            def powers(g):
                tiles = bass.ds(g * GB, GB)
                pool.wait_ge(var_ready, g + 1)
                pool.tensor_tensor(rstd, var, mhalf[:, 0:GB], ALU.pow).then_inc(rstd_ready, 1)
                pool.tensor_tensor(dis[:, tiles], deg[:, tiles], mhalf[:, 0:GB], ALU.pow).then_inc(dis_ready, 1)
                pool.wait_ge(norm_in, g + 1)
                pool.tensor_tensor(rnorm[:, tiles], norm2[:, tiles], mhalf[:, 0:GB], ALU.pow).then_inc(norm_pow, 1)

            def gather_own(q, held, source=scratch_own):
                pool.wait_ge(own_ix_ready, q + 1)
                pool.sem_inc(pool_wait_carrier, 1)
                for t in range(held * QT, (held + 1) * QT):
                    pool.indirect_dma_start(
                        own[:, t, :], None, source,
                        bass.IndirectOffsetOnAxis(ap=own_ix[:, t:t + 1], axis=0)).then_inc(own_in[held], 16)

            def gather(q, third, held, turn, slots=steps):
                pool.wait_ge(own_in[held], (turn + 1) * QT * 16)
                pool.sem_inc(pool_wait_carrier, 1)
                for b in range(QT):
                    def take_from(s):
                        ids = own[:, held * QT + b, OWN_LIST + s:OWN_LIST + s + 1].bitcast(U32)
                        pool.indirect_dma_start(
                            rows[third][:, b, s, :], None, scratch,
                            bass.IndirectOffsetOnAxis(ap=ids, axis=0)).then_inc(gathered[third], 16)
                        if s + 1 < SLOTS:
                            with pool.If(taken > s + 1):
                                take_from(s + 1)

                    taken = pool.value_load(slots[0:1, bass.ds(q * QT + b, 1)], min_val=1, max_val=SLOTS)
                    take_from(0)
                    pool.nop()

            with pool.Fori(0, NG - 1) as g:
                powers(g)
            pool.wait_ge(rows_stored, 2 * 16 * (NG - 1))
            pool.wait_ge(lists_stored, 16 * (NG - 1) + 1)
            for q in range(HELD - 2):
                gather_own(q, q, scratch_own[0:EARLY * P, :])
            powers(NG - 1)
            for q in range(HELD - 2, HELD):
                gather_own(q, q, scratch_own[0:EARLY * P, :])
            pool.wait_ge(last_rows_stored, 2 * 16)
            pool.wait_ge(first_ready, 1)
            pool.wait_ge(rows_clear, QT)
            gather(0, 0, 0, 0, first_steps)
            pool.wait_ge(last_lists_stored, 16)
            pool.wait_ge(chosen, 1)
            dense = pool.value_load(steps[0:1, NT:NT + 1], min_val=0, max_val=1)

            with pool.If(dense > 0):
                reach = pool.value_load(due_i[0:1, 0:1], min_val=16 * QT, max_val=16 * QT * SLOTS)
                for held in range(HELD):
                    pool.wait_ge(own_in[held], QT * 16)
                pool.wait_ge(gathered[0], reach)
                pool.sem_inc(first_done, 1)
                with pool.Fori(0, NQ // 2) as q2:
                    for b in range(2):
                        tiles = bass.ds((q2 * 2 + b) * QT, QT)
                        pool.wait_ge(unit_ps, q2 * 2 + 1)
                        pool.tensor_tensor(unit_f[b], nodes[:, tiles, 0:D],
                                           rnorm[:, tiles].unsqueeze(2).broadcast_to([P, QT, D]),
                                           ALU.mult).then_inc(unit_f32, 1)
                with pool.Fori(0, NG) as g:
                    pool.wait_ge(var_ready, g + NG + 1)
                    pool.tensor_tensor(rstd, var, mhalf[:, 0:GB], ALU.pow).then_inc(rstd_ready, 1)
                    pool.wait_ge(out_ready, g + 1)
                    pool.dma_start(out_groups[g], tb[:]).then_inc(stored, 16)
                    pool.wait_ge(stored, g * 16 + 16)
                    pool.sem_inc(row_free, 1)
                pool.wait_ge(stored, 16 * NG)
            with pool.Else():
                def near_pow(q):
                    pool.wait_ge(g_var, q + 1)
                    pool.tensor_tensor(rstd, var, mhalf[:, 0:GB], ALU.pow).then_inc(g_rstd, 1)

                def store(q, third):
                    pool.wait_ge(g_out, q + 1)
                    pool.sem_inc(pool_wait_carrier, 1)
                    for b in range(QT):
                        pool.indirect_dma_start(
                            out, bass.IndirectOffsetOnAxis(ap=store_ix[:, third, b:b + 1], axis=0),
                            result[third][:, b, :], None).then_inc(g_stored[third], 16)

                pool.wait_ge(rows_clear, 2 * QT)
                gather(1, 1, 1, 0)
                pool.wait_ge(total32_ps, 1)
                gather(2, 2, 2, 0)
                with pool.Fori(0, 2) as turn:
                    for k in range(HELD):
                        q = turn * HELD + k
                        near_pow(q)
                        if HELD + k + HELD < NQ:
                            gather_own(q + HELD, k)
                        else:
                            with pool.If(turn < 1):
                                gather_own(q + HELD, k)
                        gather(q + THIRDS, k % THIRDS, (k + THIRDS) % HELD, turn + (k + THIRDS) // HELD)
                        store(q, k % THIRDS)
                for q in range(2 * HELD, NQ):
                    near_pow(q)
                    if q + THIRDS < NQ:
                        gather(q + THIRDS, q % THIRDS, (q + THIRDS) % HELD, (q + THIRDS) // HELD)
                    store(q, q % THIRDS)
            pool.nop()

        @block.scalar
        def _(act):
            with act.Fori(0, NQ // 4) as q4:
                for k in range(2):
                    act.wait_ge(h_ps, q4 * 4 + k * 2 + 1)
                    for b in range(2):
                        act.wait_ge(xT_ps, q4 * 4 + k * 2 + b + 1)
                        act.activation(xT[:, k * 2 + b, :], psum[:, k * 6 + b, :], ACT.Copy).then_inc(xT_sb, 1)
            act.wait_ge(scal_ready, 1)
            act.activation(c0, neg_abs, ACT.Exp).then_inc(scal_exp, 1)
            act.activation(sig, alpha_t, ACT.Exp, scale=-1.0).then_inc(scal_exp, 1)
            act.wait_ge(negmax_ready, 1)
            for h in range(H):
                act.activation(G[:, :, D + h], G[:, :, D + h], ACT.Exp, bias=negmax[:, h:h + 1]).then_inc(e_ready, 1)
            def high(k):
                tiles = slice(k * CJ, (k + 1) * CJ)
                act.wait_ge(eh_ready, k + 1)
                act.activation(V[:, tiles, 0:WC], G[:, tiles, :], ACT.Copy).then_inc(part_hi, 1)

            high(0)
            for k in range(NT // CJ):
                if k + 1 < NT // CJ:
                    high(k + 1)
                tiles = slice(k * CJ, (k + 1) * CJ)
                act.wait_ge(rest1, k + 1)
                act.activation(V[:, tiles, WC:2 * WC], G[:, tiles, :], ACT.Copy).then_inc(part_mid, 1)
            def clear(third):
                for b in range(QT):
                    act.activation(rows[third][:, b, 1:, :], zeros[:, 0:ROW].unsqueeze(1).broadcast_to([P, SLOTS - 1, ROW]),
                                   ACT.Copy).then_inc(rows_clear, 1)

            def group(g, last, rows_in_dram, lists_in_dram):
                tiles = bass.ds(g * GB, GB)
                act.wait_ge(words_used, g + 1)
                for b in range(GB):
                    act.wait_ge(sums_ready, g * GB + b + 1)
                    act.activation(words[:, b, 0:NW], psum[:, GB + b, 0:NW], ACT.Copy).then_inc(words_free, 1)
                act.wait_ge(elu_in, g + 1)
                act.activation(tb[:], tb[:], ACT.Exp).then_inc(elu_exp, 1)
                if last:
                    clear(0)
                act.wait_ge(rows_ready, g + 1)
                act.dma_start(scratch_groups[g], nodes[:, tiles, :]).then_inc(rows_in_dram, 16)
                act.dma_start(own_groups[g][:, :, 0:ROW], nodes[:, tiles, :]).then_inc(rows_in_dram, 16)
                if last:
                    clear(1)
                act.wait_ge(lists_ready, g + 1)
                act.dma_start(own_groups[g][:, :, ROW:OWN], lists).then_inc(lists_in_dram, 16)

            with act.Fori(0, NG - 1) as g:
                group(g, False, rows_stored, lists_stored)
            group(NG - 1, True, last_rows_stored, last_lists_stored)
            act.wait_ge(chosen, 1)
            dense = act.value_load(steps[0:1, NT:NT + 1], min_val=0, max_val=1)

            def exp_scores(bank, n):
                act.wait_ge(score_ps, n + 1)
                act.activation(psum[:, GB + bank, :], psum[:, GB + bank, :], ACT.Exp, bias=neg_abs,
                               scale=beta_scale).then_inc(score_exp, 1)

            with act.If(dense > 0):
                act.wait_ge(first_done, 1)
                with act.Fori(0, NQ) as q:
                    tiles = bass.ds(q * QT, QT)
                    act.activation(xsplit[:, tiles, 0:D], nodes[:, tiles, 0:D], ACT.Copy,
                                   scale=SPLIT).then_inc(x1_hi, 1)
                with act.Fori(0, NQ // 2) as q2:
                    for b in range(2):
                        q = q2 * 2 + b
                        act.wait_ge(dx_f32, q + 1)
                        act.activation(dx[:, bass.ds(q * QT, QT), 0:D], dx_f[b][:], ACT.Copy,
                                       scale=SPLIT).then_inc(dx_hi_ready, 1)
                        act.wait_ge(unit_ps, q + 2)
                        act.activation(unit_hi[:, bass.ds(q * QT * P, QT * P)], psum[:, GB + b, :], ACT.Copy,
                                       scale=SPLIT).then_inc(unit_hi_ready, 1)
                exp_scores(0, 0)
                with act.Fori(0, NG) as g:
                    with act.Fori(0, TURNS) as turn:
                        base = act.snap((g * TURNS + turn) * CYC)
                        for k in range(CYC):
                            exp_scores((k + 1) % SB, base + k + 1)
                            act.wait_ge(edge_ready, base + k + 2)
                            act.wait_ge(split_free, base + k + 1)
                            act.activation(edge_hi[:, k % NH, :], edge[:, k % NE, :], ACT.Copy).then_inc(hi_ready, 1)
                    act.wait_ge(diff_summed, g + 2)
                    act.wait_ge(u_free, g + 1)
                    act.activation(u[:, :, 0:D + 1], acc[:, :, DC:AC], ACT.Copy).then_inc(att_copied, 1)
            with act.Else():
                def near_weights(q, third, size):
                    act.wait_ge(cos_ready, q + 1)
                    act.activation(weight[:, :, 0:size + 1], cosine[:, :, 0:size + 1], ACT.Exp, bias=neg_abs,
                                   scale=beta_t).then_inc(cos_exp, 1)
                    act.wait_ge(coef_ready, q + 1)
                    for d in range(PARTS):
                        act.wait_ge(diag_used, q * PARTS + d + 1)
                        for k in range(QT * size // PARTS):
                            b, s = divmod(d * (QT * size // PARTS) + k, size)
                            last = act.activation(diag[d % NDQ][:, k, :], ident[:], ACT.Copy,
                                                  scale=coef[third][:, b, 1 + s:2 + s])
                        last.then_inc(diag_ready, 1)

                with act.Fori(0, NQ // THIRDS) as q3:
                    for third in range(THIRDS):
                        by_size(act, q3 * THIRDS + third, lambda size: near_weights(q3 * THIRDS + third, third, size))
                by_size(act, NQ - 1, lambda size: near_weights(NQ - 1, 0, size))
            act.nop()

        @block.tensor
        def _(pe):
            pe.sem_inc(chunk_free, RING0)
            pe.sem_inc(sums_free, GB)
            pe.sem_inc(words_free, GB)
            pe.sem_inc(diag_used, NDQ)
            pe.sem_inc(near_read, THIRDS)
            pe.sem_inc(g_out_free, THIRDS)
            pe.sem_inc(lists_stored, 1)
            pe.sem_inc(split_free, NH)
            pe.sem_inc(h_ps, 3)
            for start in (unit_ps, unit_ready, dx_ready, diff_summed, att_copied, edge_ready, lo_ready, row_free,
                          words_used):
                pe.sem_inc(start, 1)
            pe.wait_ge(consts, 5)
            def turn_x(q2):
                pe.wait_ge(x_in[q2 // 2], 16)
                for b in range(2):
                    for t in range(QT):
                        last = nc.tensor.transpose(psum[:, q2 % 2 * 6 + b, t * P:(t + 1) * P],
                                                   nodes[:, (q2 * 2 + b) * QT + t, 0:D], ident[:])
                    last.then_inc(xT_ps, 1)

            turn_x(0)
            pe.wait_ge(wx_ready, 1)
            for q2 in range(NQ // 2):
                if q2 + 1 < NQ // 2:
                    turn_x(q2 + 1)
                if q2:
                    pe.wait_ge(h_sb, q2 * 2)
                for b in range(2):
                    pe.wait_ge(xT_sb, q2 * 2 + b + 1)
                    for t in range(QT):
                        c = (t % 2) * 256
                        last = nc.tensor.matmul(psum[:, 2 + 2 * b + t // 2, c:c + WC],
                                                xT[:, q2 % 2 * 2 + b, t * P:(t + 1) * P], Wx[:], start=True, stop=True)
                    last.then_inc(h_ps, 1)
            pe.wait_ge(h_sb, NQ)
            pe.wait_ge(consts, 6 + BITS)

            def turn_and_spread(columns, n, turned, spread, done):
                nc.tensor.transpose(psum[0:n, 6, 0:P], columns, ident[:]).then_inc(turned, 1)
                pe.wait_ge(peaks_ready, spread)
                nc.tensor.matmul(psum[:, 7, 0:n], ones_k[0:n, :], peaks[0:n, 0:n], start=True, stop=True).then_inc(done, 1)

            pe.wait_ge(smax_ready, 1)
            turn_and_spread(smax, H, smax_turned, 1, gmax_ready)

            def sweep(bank, cols, first):
                return nc.tensor.matmul(psum[:, bank, 0:cols], zeros[:, 0:P], zeros[:, 0:cols],
                                        start=first, stop=not first, skip_group_check=True)

            def neighbour_sums(g, turn, first, end):
                for s in range(RING0):
                    pe.wait_ge(table_ready, turn * RING0 + s + 1)
                    pe.wait_ge(chunk_in[s], (g * TURNS0 + turn + 1) * 16)
                    for b in range(GB):
                        if first and s == 0:
                            pe.wait_ge(sums_free, g * GB + b + 1)
                            pe.wait_ge(words_free, g * GB + b + 1)
                        for t in range(CJ):
                            adj_ji = ring0_bf[s][:, t, b * P:(b + 1) * P, 1]
                            nc.tensor.matmul(psum[:, b, 0:VC], adj_ji, V[:, (turn * RING0 + s) * CJ + t, 0:VC],
                                             start=first and s == 0 and t == 0,
                                             stop=end and s == RING0 - 1 and t == CJ - 1, skip_group_check=True)
                            last = nc.tensor.matmul(psum[:, GB + b, bass.ds(((turn * RING0 + s) * CJ + t) * WPT, WPT)],
                                                    adj_ji, bits[:], start=True, stop=True, skip_group_check=True)
                        if end and s == RING0 - 1:
                            if b == GB - 1:
                                last.then_inc(chunk_free, 1)
                                last = sweep(b, 1, False)
                            last.then_inc(sums_ready, 1)
                        elif b == GB - 1:
                            last.then_inc(chunk_free, 1)

            with pe.Fori(0, NG) as g:
                neighbour_sums(g, 0, True, False)
                for turn in range(1, TURNS0):
                    neighbour_sums(g, turn, False, turn == TURNS0 - 1)
            pe.wait_ge(first_counted, 1)
            pe.wait_ge(words_free, NG * GB + GB)
            turn_and_spread(longest[:, 0:QT], QT, first_turned, 2, first_max)
            pe.wait_ge(counted, 1)
            turn_and_spread(longest[:], NT + 1, counts_turned, 3, counts_max)
            pe.wait_ge(chosen, 1)
            dense = pe.value_load(steps[0:1, NT:NT + 1], min_val=0, max_val=1)
            with pe.If(dense > 0):
                pe.wait_ge(x1_lo, NG)
                pe.wait_ge(sums_free, NG * GB + GB)
                sweep(0, D, True)
                with pe.Fori(0, NQ) as q:
                    for t in range(QT):
                        for part in (0, D + 1):
                            nc.tensor.matmul(psum[:, 0, 0:D], ones16[:], xsplit[:, q * QT + t, part:part + D],
                                             start=False, stop=False, skip_group_check=True)
                sweep(0, D, False).then_inc(total_ps, 1)
                with pe.Fori(0, NQ // 2) as q2:
                    pe.wait_ge(unit_ready, q2 * 2 + 1)
                    for b in range(2):
                        pe.wait_ge(unit_f32, q2 * 2 + b + 1)
                        for t in range(QT):
                            last = nc.tensor.transpose(psum[:, GB + b, t * P:(t + 1) * P], unit_f[b][:, t, :], ident[:])
                        last.then_inc(unit_ps, 1)
                pe.wait_ge(unit_ready, NQ + 1)
                pe.wait_ge(dx_ready, NQ + 1)
                pe.wait_ge(total_read, 1)

                def scores(bank, tile, group):
                    hi_j, lo_j = (part[:, bass.ds(tile * P, P)] for part in (unit_hi, unit_lo))
                    hi_i, lo_i = (part[:, bass.ds(group * GW, GW)] for part in (unit_hi, unit_lo))
                    nc.tensor.matmul(psum[:, GB + bank, :], hi_j, hi_i, start=True, stop=False)
                    nc.tensor.matmul(psum[:, GB + bank, :], hi_j, lo_i, start=False, stop=False)
                    nc.tensor.matmul(psum[:, GB + bank, :], lo_j, hi_i, start=False, stop=True).then_inc(score_ps, 1)

                for n in range(AHEAD):
                    scores(n, n, 0)
                with pe.Fori(0, NG) as g:
                    pe.wait_ge(diff_summed, g + 1)
                    pe.wait_ge(att_copied, g + 1)
                    for b in range(GB):
                        sweep(b, AC, True)
                    with pe.Fori(0, TURNS) as turn:
                        base = pe.snap((g * TURNS + turn) * CYC)
                        next_turn = pe.snap((turn + 1) % TURNS)
                        next_group = pe.snap((g + (turn + 1) // TURNS) % NG)
                        for s in range(RING):
                            pe.wait_ge(chunk_in[s], (g * TURNS + turn + LOADS0 + 1) * 16)
                            for t in range(CJ):
                                k = s * CJ + t
                                pe.wait_ge(edge_ready, base + k + 1)
                                if k + AHEAD < CYC:
                                    scores((k + AHEAD) % SB, turn * CYC + k + AHEAD, g)
                                else:
                                    scores((k + AHEAD) % SB, next_turn * CYC + k + AHEAD - CYC, next_group)
                                j = turn * CYC + k
                                for b in range(GB):
                                    nc.tensor.matmul(psum[:, b, 0:DC], ring_bf[:, s, t, b * P:(b + 1) * P, 1],
                                                     dx[:, j, :], start=False, stop=False, skip_group_check=True)
                                pe.wait_ge(lo_ready, base + k + 2)
                                for b in range(GB):
                                    w_hi = edge_hi[:, k % NH, b * P:(b + 1) * P]
                                    w_lo = edge_lo[:, k % NH, b * P:(b + 1) * P]
                                    first = nc.tensor.matmul(psum[:, b, DC:AC], w_hi, xsplit[:, j, 0:D + 1],
                                                             start=False, stop=False, skip_group_check=True)
                                    if t == CJ - 1 and b == 0:
                                        first.then_inc(chunk_free, 1)
                                    nc.tensor.matmul(psum[:, b, DC:DC + D], w_hi, xsplit[:, j, D + 1:2 * D + 1],
                                                     start=False, stop=False, skip_group_check=True)
                                    last = nc.tensor.matmul(psum[:, b, DC:AC], w_lo, xsplit[:, j, 0:D + 1],
                                                            start=False, stop=False, skip_group_check=True)
                                last.then_inc(split_free, 1)
                    for b in range(GB):
                        last = sweep(b, AC, False)
                    last.then_inc(acc_ready, 1)
            with pe.Else():
                sweep(7, D, True)
                with pe.Fori(0, NQ) as q:
                    for t in range(QT):
                        nc.tensor.matmul(psum[:, 7, 0:D], ones32, nodes[:, q * QT + t, 0:D],
                                         start=False, stop=False, skip_group_check=True)
                sweep(7, D, False).then_inc(total32_ps, 1)
                pe.wait_ge(total32_read, 1)

                def near_sums(q, third, size):
                    pe.wait_ge(near_read, q + 1)
                    for d in range(PARTS):
                        pe.wait_ge(diag_ready, q * PARTS + d + 1)
                        for k in range(QT * size // PARTS):
                            b, s = divmod(d * (QT * size // PARTS) + k, size)
                            last = nc.tensor.matmul(psum[:, third, b * D:(b + 1) * D], diag[d % NDQ][:, k, :],
                                                    rows[third][:, b, s, 0:D], start=s == 0, stop=s == size - 1)
                        last.then_inc(diag_used, 1)

                with pe.Fori(0, NQ // THIRDS) as q3:
                    for third in range(THIRDS):
                        by_size(pe, q3 * THIRDS + third, lambda size: near_sums(q3 * THIRDS + third, third, size))
                by_size(pe, NQ - 1, lambda size: near_sums(NQ - 1, 0, size))
            pe.nop()

        @block.vector
        def _(dve):
            v = nc.vector

            class Chain:
                def __init__(self, sem):
                    self.sem, self.base, self.n = sem, 0, 0

                def start(self, base):
                    self.base, self.n = base, 0

                def __call__(self, ins, settle=False):
                    self.n += 1
                    ins.then_inc(self.sem, 1)
                    dve.wait_ge(self.sem, self.base + self.n)
                    if settle:
                        settled()

            def settled():
                dve.sem_inc(wait_carrier, 1)

            link = Chain(dve_chain)

            def per_tile(ap):
                return ap.unsqueeze(2).broadcast_to([P, GB, D])

            def all_tiles(ap):
                return ap.unsqueeze(1).broadcast_to([P, GB, D])

            v.memset(V[:, :, 3 * WC], 1.0)
            link(v.memset(ones_k, 1.0))
            dve.wait_ge(ids_ready, 1)
            v.tensor_copy(node_id[:], due_i[:])
            dve.wait_ge(w_in, 16)
            dve.wait_ge(a_in, 16)
            link(v.tensor_tensor(ta[:, 0, :], Wx[:, 0:D], a_bc[:], ALU.mult))
            v.tensor_reduce(Wx[:, D:WC], ta[:, 0, :].rearrange("p (h d) -> p h d", h=H), AX_X,
                            ALU.add).then_inc(wx_ready, 1)
            dve.wait_ge(ab_in, 32)
            link(v.tensor_scalar(neg_beta, beta_t, -1.0, None, ALU.mult))
            v.tensor_scalar(beta_scale, beta_t, 1.0 / (SPLIT * SPLIT), None, ALU.mult)
            v.tensor_tensor(neg_abs, beta_t, neg_beta, ALU.min).then_inc(scal_ready, 1)
            with dve.Fori(0, NQ // 2) as q2:
                for b in range(2):
                    q = q2 * 2 + b
                    dve.wait_ge(h_ps, q + 4)
                    h_quad = psum[:, 2 + 2 * b:4 + 2 * b, :].rearrange("p k (t c) -> p (k t) c", c=256)
                    v.tensor_copy(G[:, bass.ds(q * QT, QT), :], h_quad[:, :, 0:WC]).then_inc(h_sb, 1)
            dve.wait_ge(h_sb, NQ)
            v.tensor_reduce(smax, G[:, :, D:WC].rearrange("p t h -> p h t"), AX_X, ALU.max).then_inc(smax_ready, 1)

            def over_partitions(n, turned):
                dve.wait_ge(turned, 1)
                link(v.tensor_reduce(peak[0:n], psum[0:n, 6, 0:P], AX_X, ALU.max))
                v.tensor_scalar(peaks[0:n, 0:n], ident[0:n, 0:n], peak[0:n], None, ALU.mult).then_inc(peaks_ready, 1)

            over_partitions(H, smax_turned)
            dve.wait_ge(gmax_ready, 1)
            v.tensor_scalar(negmax, psum[:, 7, 0:H], -1.0, None, ALU.mult).then_inc(negmax_ready, 1)
            dve.wait_ge(e_ready, H)

            def times_e(k):
                tiles = slice(k * CJ, (k + 1) * CJ)
                h_view = G[:, tiles, 0:D].rearrange("p t (h d) -> p t h d", h=H)
                v.tensor_tensor(h_view, h_view, G[:, tiles, D:WC].unsqueeze(3).broadcast_to([P, CJ, H, DH]),
                                ALU.mult).then_inc(eh_ready, 1)

            def rest_of(k):
                tiles = slice(k * CJ, (k + 1) * CJ)
                dve.wait_ge(part_hi, k + 1)
                v.tensor_tensor(G[:, tiles, :], G[:, tiles, :], V[:, tiles, 0:WC], ALU.subtract).then_inc(rest1, 1)

            def part_low(k):
                tiles = slice(k * CJ, (k + 1) * CJ)
                dve.wait_ge(part_mid, k + 1)
                v.tensor_tensor(V[:, tiles, 2 * WC:3 * WC], G[:, tiles, :], V[:, tiles, WC:2 * WC],
                                ALU.subtract).then_inc(table_ready, 1)

            times_e(0)
            times_e(1)
            rest_of(0)
            for k in range(1, NT // CJ):
                if k + 1 < NT // CJ:
                    times_e(k + 1)
                rest_of(k)
                part_low(k - 1)
            part_low(NT // CJ - 1)
            dve.wait_ge(table_ready, NT // CJ)
            link(v.memset(ones32, 1.0))
            dve.wait_ge(scal_exp, 2)
            link(v.tensor_scalar(sig, sig, 1.0, None, ALU.add))
            link(v.reciprocal(sig, sig))
            v.tensor_scalar(sig_s, sig, 1.0 / SPLIT, None, ALU.mult)
            v.tensor_scalar(neg_sig, sig, -1.0, None, ALU.mult)
            link(v.tensor_scalar(n_c0, c0, float(N), None, ALU.mult))

            FIRST = link.n

            def centre(y, link, done):
                link(v.tensor_reduce(mean, y, AX_X, ALU.add))
                link(v.tensor_scalar(mean, mean, -1.0 / D, None, ALU.mult))
                link(v.tensor_tensor(ta[:], y, per_tile(mean), ALU.add))
                link(v.tensor_tensor(tb[:], ta[:], ta[:], ALU.mult))
                link(v.tensor_reduce(ss, tb[:], AX_X, ALU.add))
                v.tensor_scalar(var, ss, 1.0 / D, LN_EPS, ALU.mult, ALU.add).then_inc(done, 1)

            def quotient_and_norm(g, tiles):
                for b in range(GB):
                    dve.wait_ge(sums_ready, g * GB + b + 1)
                    v.tensor_scalar(degree[:, bass.ds(g * GB + b, 1)], psum[:, b, 3 * WC:3 * WC + 1], 1.0, None, ALU.mult)
                    v.tensor_reduce(u[:, b, :], psum[:, b, 0:3 * WC].rearrange("p (k c) -> p c k", k=3), AX_X,
                                    ALU.add).then_inc(sums_free, 1)
                dve.wait_ge(sums_free, (g + 2) * GB)
                link(v.reciprocal(rden[:], u[:, :, D:WC]))
                for h in range(H):
                    ins = v.tensor_tensor(ta[:, :, h * DH:(h + 1) * DH], u[:, :, h * DH:(h + 1) * DH],
                                          rden[:, :, h].unsqueeze(2).broadcast_to([P, GB, DH]), ALU.mult)
                link(ins)
                link(v.tensor_tensor(ta[:], ta[:], all_tiles(bias_bc[:]), ALU.add))
                v.tensor_scalar(tb[:], ta[:], 0.0, None, ALU.min).then_inc(elu_in, 1)
                v.tensor_scalar(deg[:, tiles], counts_deg(tiles), 1.0, None, ALU.max)
                link(v.scalar_tensor_tensor(out=tc[:], in0=ta[:], scalar=0.0, in1=nodes[:, tiles, 0:D],
                                            op0=ALU.max, op1=ALU.add))
                dve.wait_ge(elu_exp, g + 1)
                link(v.scalar_tensor_tensor(out=tc[:], in0=tb[:], scalar=-1.0, in1=tc[:],
                                            op0=ALU.add, op1=ALU.add))
                centre(tc[:], link, var_ready)
                dve.wait_ge(rstd_ready, g + 1)
                v.tensor_tensor(nodes[:, tiles, 0:D], ta[:], per_tile(rstd), ALU.mult)
                link(v.tensor_tensor(nn, ss, rstd, ALU.mult))
                v.tensor_tensor(norm2[:, tiles], nn, rstd, ALU.mult).then_inc(norm_in, 1)

            def list_neighbours(g, tiles):
                dve.wait_ge(words_free, (g + 2) * GB)
                settled()
                for b in range(GB):
                    row, lo, hi = words[:, b, 0:NW], b * SLOTS, b * SLOTS + 8
                    link(v.max(out=w_val[:, lo:lo + 8], in_=row), settle=True)
                    v.max_index(out=w_at[:, lo:lo + 8], in_max=w_val[:, lo:lo + 8], in_values=row)
                    link(v.match_replace(out=row, in_to_replace=w_val[:, lo:lo + 8], in_values=row, imm_value=0.0), settle=True)
                    link(v.max(out=w_val[:, hi:hi + 8], in_=row), settle=True)
                    ins = v.max_index(out=w_at[:, hi:hi + 8], in_max=w_val[:, hi:hi + 8], in_values=row)
                ins.then_inc(words_used, 1)
                dve.wait_ge(words_used, g + 2)
                link(v.tensor_scalar(w_base, w_at, float(BITS), None, ALU.mult))
                by_level = found.rearrange("p (b l s) -> p b l s", l=LEVELS, s=SLOTS)
                for level in range(LEVELS):
                    v.tensor_scalar(w_exp, w_val.bitcast(I32), 23, None, ALU.logical_shift_right)
                    link(v.tensor_scalar(w_top, w_val.bitcast(I32), 0x7F800000, None, ALU.bitwise_and))
                    key = by_level[:, :, level, :]
                    four = lambda ap: ap.rearrange("p (b s) -> p b s", s=SLOTS)
                    link(v.scalar_tensor_tensor(out=key, in0=four(w_exp), scalar=-126.0, in1=four(w_base),
                                                op0=ALU.add, op1=ALU.add))
                    link(v.scalar_tensor_tensor(out=key, in0=four(w_val), scalar=0.0, in1=key, op0=ALU.is_gt,
                                                op1=ALU.mult))
                    link(v.tensor_tensor(w_val, w_val, w_top.bitcast(F32), ALU.subtract))
                for b in range(GB):
                    part = found[:, b * LEVELS * SLOTS:(b + 1) * LEVELS * SLOTS]
                    link(v.scalar_tensor_tensor(out=part, in0=part, scalar=node_q[:, b:b + 1], in1=part,
                                                op0=ALU.not_equal, op1=ALU.mult), settle=True)
                for b in range(GB):
                    part = found[:, b * LEVELS * SLOTS:(b + 1) * LEVELS * SLOTS]
                    lo, hi = b * SLOTS, b * SLOTS + 8
                    link(v.max(out=key_q[:, lo:lo + 8], in_=part), settle=True)
                    link(v.match_replace(out=part, in_to_replace=key_q[:, lo:lo + 8], in_values=part, imm_value=0.0), settle=True)
                    ins = v.max(out=key_q[:, hi:hi + 8], in_=part)
                link(ins)
                kq = key_q.rearrange("p (b s) -> p b s", s=SLOTS)
                dve.wait_ge(lists_stored, g * 16 + 1)
                v.tensor_tensor(lists[:, :, 0], norm2[:, tiles], rnorm[:, tiles], ALU.mult)
                link(v.tensor_scalar(is_slot, kq, 0.0, None, ALU.is_gt))
                v.tensor_reduce(counts[:, tiles], is_slot, AX_X, ALU.add)
                ids = node_q[:].unsqueeze(2).broadcast_to([P, GB, SLOTS])
                wb = w_base.rearrange("p (b s) -> p b s", s=SLOTS)
                link(v.tensor_tensor(wb, is_slot, ids, ALU.mult))
                link(v.tensor_tensor(wb, ids, wb, ALU.subtract))
                v.scalar_tensor_tensor(out=list_u, in0=wb, scalar=-1.0, in1=kq, op0=ALU.add,
                                       op1=ALU.add).then_inc(lists_ready, 1)

            def counts_deg(tiles):
                return degree[:, tiles]

            def dense_layer():
                dve.wait_ge(first_done, 1)
                v.memset(xsplit[:, :, D], 1.0)
                with dve.Fori(0, NQ) as q:
                    tiles = bass.ds(q * QT, QT)
                    dve.wait_ge(x1_hi, q + 1)
                    v.scalar_tensor_tensor(out=xsplit[:, tiles, D + 1:2 * D + 1], in0=nodes[:, tiles, 0:D], scalar=SPLIT,
                                           in1=xsplit[:, tiles, 0:D], op0=ALU.mult,
                                           op1=ALU.subtract).then_inc(x1_lo, 1)
                with dve.Fori(0, NQ // 2) as q2:
                    dve.wait_ge(dx_ready, q2 * 2 + 1)
                    for b in range(2):
                        q = q2 * 2 + b
                        tiles = bass.ds(q * QT, QT)
                        v.tensor_tensor(dx_f[b][:], nodes[:, tiles, 0:D],
                                        dis[:, tiles].unsqueeze(2).broadcast_to([P, QT, D]), ALU.mult).then_inc(dx_f32, 1)
                    for b in range(2):
                        q = q2 * 2 + b
                        tiles = bass.ds(q * QT, QT)
                        cols = bass.ds(q * QT * P, QT * P)
                        dve.wait_ge(dx_hi_ready, q + 1)
                        v.scalar_tensor_tensor(out=dx[:, tiles, D:DC], in0=dx_f[b][:], scalar=SPLIT, in1=dx[:, tiles, 0:D],
                                               op0=ALU.mult, op1=ALU.subtract).then_inc(dx_ready, 1)
                        dve.wait_ge(unit_hi_ready, q + 1)
                        v.scalar_tensor_tensor(out=unit_lo[:, cols], in0=psum[:, GB + b, :], scalar=SPLIT,
                                               in1=unit_hi[:, cols], op0=ALU.mult,
                                               op1=ALU.subtract).then_inc(unit_ready, 1)
                dve.wait_ge(total_ps, 1)
                v.tensor_scalar(total_bc[:], psum[:, 0, 0:D], c0, None, ALU.mult).then_inc(total_read, 1)
                dve.wait_ge(total_read, 1)
                dve.wait_ge(unit_ready, NQ + 1)
                dve.sem_inc(u_free, 1)
                link1 = Chain(dve_chain1)
                with dve.Fori(0, NG) as g:
                    with dve.Fori(0, TURNS) as turn:
                        base = dve.snap((g * TURNS + turn) * CYC)

                        def masked(k):
                            if k % CJ == 0:
                                dve.wait_ge(chunk_in[k // CJ], (g * TURNS + turn + LOADS0 + 1) * 16)
                            if k == 0 or k >= NE:
                                dve.wait_ge(lo_ready, base + max(k - NE + 1, 0) + 1)
                            dve.wait_ge(score_exp, base + k + 1)
                            v.scalar_tensor_tensor(out=edge[:, k % NE, :], in0=psum[:, GB + k % SB, :], scalar=c0,
                                                   in1=ring[:, k // CJ, k % CJ, :], op0=ALU.subtract,
                                                   op1=ALU.mult).then_inc(edge_ready, 1)

                        masked(0)
                        for k in range(CYC):
                            if k + 1 < CYC:
                                masked(k + 1)
                            dve.wait_ge(hi_ready, base + k + 1)
                            v.tensor_tensor(edge_lo[:, k % NH, :], edge[:, k % NE, :], edge_hi[:, k % NH, :],
                                            ALU.subtract).then_inc(lo_ready, 1)
                    link1.start(dve.snap(g * LINKS1))
                    tiles = bass.ds(g * GB, GB)
                    dve.wait_ge(acc_ready, g + 1)
                    v.tensor_reduce(ta[:], acc[:, :, 0:DC].rearrange("p b (k c) -> p b c k", k=2), AX_X,
                                    ALU.add).then_inc(diff_summed, 1)
                    dve.wait_ge(att_copied, g + 2)
                    link1(v.tensor_scalar(nn, u[:, :, D], n_c0, None, ALU.add))
                    link1(v.reciprocal(nn, nn))
                    v.tensor_scalar(mean, dis[:, tiles], 1.0 / SPLIT, None, ALU.mult)
                    link1(v.tensor_scalar(nn, nn, sig_s, None, ALU.mult))
                    dve.wait_ge(row_free, g + 1)
                    v.tensor_tensor(tb[:], u[:, :, 0:D], all_tiles(total_bc[:]), ALU.add).then_inc(u_free, 1)
                    dve.wait_ge(u_free, g + 2)
                    link1(v.tensor_tensor(tb[:], tb[:], per_tile(nn), ALU.mult))
                    dve.wait_ge(diff_summed, g + 2)
                    link1(v.tensor_tensor(ta[:], ta[:], per_tile(mean), ALU.mult))
                    link1(v.tensor_tensor(ta[:], ta[:], tb[:], ALU.add))
                    link1(v.scalar_tensor_tensor(out=tc[:], in0=nodes[:, tiles, 0:D], scalar=neg_sig, in1=ta[:],
                                                op0=ALU.mult, op1=ALU.add))
                    centre(tc[:], link1, var_ready)
                    dve.wait_ge(rstd_ready, g + NG + 1)
                    v.tensor_tensor(tb[:], ta[:], per_tile(rstd), ALU.mult).then_inc(out_ready, 1)
                    assert link1.n == LINKS1, link1.n

            def gathered_layer():
                near = Chain(dve_chain1)

                def own_tiles(q):
                    return bass.ds(q % HELD * QT, QT)

                def own_part(q, b, n):
                    return bass.ds(q % HELD * QT + b, n)

                def coefficients(q, third, base, size):
                    near.start(base)
                    near_rows, mine, all_slots = rows[third], own[:, own_tiles(q), :], slice(0, size + 1)
                    together = SLOTS // size
                    for k, b in enumerate(range(0, QT, together)):
                        tiles = slice(b, b + together)
                        products = prod[k % 2].rearrange("p (t s) d -> p t s d", t=together)
                        near(v.tensor_tensor(products, near_rows[:, tiles, 0:size, 0:D],
                                             own[:, own_part(q, b, together), 0:D].unsqueeze(2).broadcast_to(
                                                 [P, together, size, D]), ALU.mult))
                        ins = v.tensor_reduce(cosine[:, tiles, 1:size + 1], products, AX_X, ALU.add)
                    near(ins)

                    def per_slot(ap):
                        return ap.unsqueeze(2).broadcast_to([P, QT, size + 1])

                    near(v.tensor_tensor(cosine[:, :, 1:size + 1], cosine[:, :, 1:size + 1], near_rows[:, :, 0:size, D],
                                         ALU.mult))
                    near(v.tensor_scalar(cosine[:, :, 0], mine[:, :, OWN_ABS], 1.0, None, ALU.mult))
                    v.tensor_tensor(cosine[:, :, all_slots], cosine[:, :, all_slots], per_slot(mine[:, :, D]),
                                    ALU.mult).then_inc(cos_ready, 1)
                    taken = mine[:, :, OWN_IS:OWN_IS + size + 1]
                    near(v.tensor_tensor(hop[:, :, 1:size + 1], near_rows[:, :, 0:size, D + 1], taken[:, :, 1:size + 1],
                                         ALU.mult))
                    near(v.tensor_scalar(hop[:, :, 0], mine[:, :, D + 1], 1.0, None, ALU.mult))
                    near(v.tensor_tensor(hop[:, :, all_slots], hop[:, :, all_slots], per_slot(mine[:, :, D + 1]),
                                         ALU.mult))
                    dve.wait_ge(cos_exp, q + 1)
                    w = weight[:, :, all_slots]
                    near(v.scalar_tensor_tensor(out=w, in0=w, scalar=c0, in1=taken, op0=ALU.subtract, op1=ALU.mult))
                    share = quotient[:, third, :]
                    near(v.tensor_reduce(share, w, AX_X, ALU.add))
                    near(v.tensor_scalar(share, share, n_c0, None, ALU.add))
                    near(v.reciprocal(share, share))
                    near(v.tensor_scalar(share, share, sig, None, ALU.mult))
                    near(v.tensor_tensor(w, w, per_slot(share), ALU.mult))
                    near(v.tensor_tensor(coef[third][:, :, all_slots], w, hop[:, :, all_slots], ALU.add))
                    v.tensor_scalar(coef[third][:, :, 0], coef[third][:, :, 0], sig, None,
                                    ALU.subtract).then_inc(coef_ready, 1)
                    assert near.n <= LINKS_A, near.n
                    if near.n < LINKS_A:
                        dve.sem_inc(dve_chain1, LINKS_A - near.n)

                def weigh(q, third, base):
                    reach = dve.value_load(due_i[0:1, bass.ds(q, 1)], min_val=16 * QT,
                                           max_val=16 * QT * SLOTS * (NQ // THIRDS + 1))

                    def quad(size):
                        dve.wait_ge(gathered[third], reach)
                        coefficients(q, third, base, size)

                    by_size(dve, q, quad)

                def finish(q, third, base):
                    near.start(base)
                    dve.wait_ge(coef_ready, q + 1)
                    near(v.tensor_tensor(ta[:], own[:, own_tiles(q), 0:D], per_tile(coef[third][:, :, 0]), ALU.mult))
                    near(v.tensor_tensor(tb[:], all_tiles(total_bc[:]), per_tile(quotient[:, third, :]), ALU.mult))
                    near(v.tensor_tensor(ta[:], ta[:], tb[:], ALU.add))
                    dve.wait_ge(diag_used, q * PARTS + PARTS + NDQ)
                    sums = psum[:, third, :].rearrange("p (b d) -> p b d", d=D)
                    v.tensor_tensor(tc[:], ta[:], sums, ALU.add).then_inc(near_read, 1)
                    dve.wait_ge(near_read, q + THIRDS + 1)
                    centre(tc[:], near, g_var)
                    dve.wait_ge(g_out_free, q + 1)
                    v.tensor_copy(store_ix[:, third, :], node_ix[:, bass.ds(q * QT, QT)].bitcast(U32))
                    dve.wait_ge(g_rstd, q + 1)
                    v.tensor_tensor(result[third], ta[:], per_tile(rstd), ALU.mult).then_inc(g_out, 1)
                    assert near.n == LINKS_B, near.n

                dve.wait_ge(total32_ps, 1)
                v.tensor_scalar(total_bc[:], psum[:, 7, 0:D], c0, None, ALU.mult).then_inc(total32_read, 1)
                dve.wait_ge(total32_read, 1)
                LINKS_AB = LINKS_A + LINKS_B
                weigh(0, 0, 0)
                with dve.Fori(0, NQ // THIRDS) as q3:
                    for third in range(THIRDS):
                        q = q3 * THIRDS + third
                        base = dve.snap(q * LINKS_AB + LINKS_A)
                        next_own((q + HELD) % NQ, q % HELD)
                        weigh(q + 1, (third + 1) % THIRDS, base)
                        finish(q, third, base + LINKS_A)
                dve.wait_ge(g_out, NQ - 1)
                finish(NQ - 1, 0, (NQ - 1) * LINKS_AB + LINKS_A)

            def next_own(q, held):
                v.tensor_copy(own_ix[:, bass.ds(held * QT, QT)],
                              node_ix[:, bass.ds(q * QT, QT)].bitcast(U32)).then_inc(own_ix_ready, 1)

            dve.wait_ge(bias_in, 16)
            v.memset(lists[:, :, 1], 1.0)

            def group(g):
                tiles = bass.ds(g * GB, GB)
                quotient_and_norm(g, tiles)
                v.tensor_copy(node_q[:], node_id[:, tiles])
                dve.wait_ge(norm_pow, g + 1)
                dve.wait_ge(dis_ready, g + 1)
                v.tensor_scalar(rnorm[:, tiles], rnorm[:, tiles], 1.0 / NORM_FLOOR, None,
                                ALU.min).then_inc(rows_ready, 1)

            def place_keys(tiles):
                link(v.scalar_tensor_tensor(out=places[:, tiles], in0=counts[:, tiles], scalar=float(N),
                                            in1=node_id[:, tiles], op0=ALU.mult, op1=ALU.add))

            def decode(places, mask):
                link(v.tensor_scalar(order_i[:, places], order[:, places], -1.0, None, ALU.add))
                v.tensor_scalar(node_ix[:, places], order_i[:, places], N - 1, None, ALU.bitwise_and)
                link(v.tensor_scalar(order_i[:, places], order_i[:, places], N.bit_length() - 1, mask,
                                     ALU.logical_shift_right, ALU.bitwise_and))
                return v.tensor_copy(longest[:, places], order_i[:, places])

            with dve.Fori(0, NG - 1) as g:
                link.start(dve.snap(g * LINKS0 + FIRST))
                group(g)
                dve.wait_ge(rows_ready, g + 1)
                list_neighbours(g, bass.ds(g * GB, GB))
                assert link.n == LINKS0, link.n
            link.start((NG - 1) * LINKS0 + FIRST)
            early, first = slice(0, EARLY), HELD * QT
            place_keys(early)
            link(v.tensor_copy(due[:, early], places[:, early]))
            for k in range(0, first, 8):
                link(v.max(out=order[:, k:k + 8], in_=due[:, early]))
                if k + 8 < first:
                    link(v.match_replace(out=due[:, early], in_to_replace=order[:, k:k + 8], in_values=due[:, early],
                                         imm_value=0.0))
            decode(slice(0, first), AHEAD_OF_ALL - 1).then_inc(first_counted, 1)
            for q in range(HELD):
                next_own(q, q)
            link(v.tensor_scalar(due[:, early], places[:, early], order[:, first - 1:first], float(AHEAD_OF_ALL * N),
                                 ALU.is_ge, ALU.mult))
            link(v.tensor_tensor(places[:, early], places[:, early], due[:, early], ALU.add))
            group(NG - 1)
            link(v.memset(ones_k, 1.0))
            over_partitions(QT, first_turned)
            dve.wait_ge(first_max, 1)
            v.tensor_scalar(first_steps, psum[:, 7, 0:QT], 1.0, None, ALU.max).then_inc(first_ready, 1)
            dve.wait_ge(rows_ready, NG)
            list_neighbours(NG - 1, slice(EARLY, NT))
            link(v.scalar_tensor_tensor(out=due[:], in0=counts[:], scalar=1.0, in1=degree[:], op0=ALU.add,
                                        op1=ALU.not_equal))
            v.tensor_reduce(longest[:, NT:NT + 1], due[:], AX_X, ALU.max)
            place_keys(slice(EARLY, NT))
            for k in range(0, NT, 8):
                link(v.max(out=order[:, k:k + 8], in_=places))
                if k + 8 < NT:
                    link(v.match_replace(out=places, in_to_replace=order[:, k:k + 8], in_values=places, imm_value=0.0))
            decode(slice(0, NT), AHEAD_OF_ALL - 1).then_inc(counted, 1)
            over_partitions(NT + 1, counts_turned)
            dve.wait_ge(counts_max, 1)
            link(v.tensor_scalar(due[:], most[:, 0:NT], 1.0, None, ALU.max))
            v.tensor_copy(steps[:, 0:NT], due[:])
            v.tensor_copy(steps[:, NT:NT + 1], most[:, NT:NT + 1])
            link(v.tensor_reduce(counts[:, 0:NQ], due[:].rearrange("p (q t) -> p q t", t=QT), AX_X, ALU.add))
            link(v.tensor_scalar(counts[:, 0:NQ], counts[:, 0:NQ], 16.0, None, ALU.mult))
            for q in range(THIRDS, NQ, THIRDS):
                end = min(q + THIRDS, NQ)
                link(v.tensor_tensor(counts[:, q:end], counts[:, q:end], counts[:, q - THIRDS:end - THIRDS], ALU.add))
            v.tensor_copy(due_i[:, 0:NQ], counts[:, 0:NQ]).then_inc(chosen, 1)
            dve.wait_ge(chosen, 1)
            dense = dve.value_load(steps[0:1, NT:NT + 1], min_val=0, max_val=1)

            with dve.If(dense > 0):
                dense_layer()
            with dve.Else():
                gathered_layer()
            dve.nop()


_INS = ['x', 'adj', 'L0_gnn_W', 'L0_gnn_a_self', 'L0_gnn_a_neigh', 'L0_gnn_bias', 'L1_gnn_t', 'L1_gnn_alpha',
        'L1_gnn_beta']


def kernel(**inputs):
    import numpy as _np
    import concourse.bacc as _bacc
    from concourse import mybir as _mybir
    from concourse.bass_utils import run_bass_kernel_spmd as _run

    nc = _bacc.Bacc("TRN2", target_bir_lowering=False, num_devices=1)
    arrays, args = {}, []
    for name in _INS:
        a = _np.ascontiguousarray(inputs[name])
        if a.size == 1:
            a = a.reshape(1, 1)
        arrays[f"in_{name}_dram"] = a
        args.append(nc.dram_tensor(f"in_{name}_dram", a.shape, _mybir.dt.from_np(a.dtype), kind="ExternalInput").ap())
    out = nc.dram_tensor("out_0_dram", inputs["x"].shape, F32, kind="ExternalOutput").ap()
    graph_layers_kernel(nc, *args, out)
    r = _run(nc, [arrays], core_ids=[0])
    return r.results[0]["out_0_dram"]
```
